# Optimizing a Trainium2 kernel written in Bass

```python
import numpy as np
import jax
import jax.numpy as jnp

def _softmax(x, axis=-1):
    return jax.nn.softmax(x, axis=axis)

def _gelu(x):
    return jax.nn.gelu(x, approximate=True)

def _silu(x):
    return jax.nn.silu(x)

def _sigmoid(x):
    return jax.nn.sigmoid(x)

def _layernorm(x, axis=-1, eps=1e-05):
    m = jnp.mean(x, axis=axis, keepdims=True)
    v = jnp.var(x, axis=axis, keepdims=True)
    return (x - m) / jnp.sqrt(v + eps)

def _scatter_add(tgt, idx, src, axis=0):
    return tgt.at[idx].add(src)

def _segment_sum(src, seg, n):
    return jax.ops.segment_sum(src, seg, n)
kernel_name = 'mk_gnn_preln_d1_gnn_r64_0878eb'

def setup_inputs(seed: int=0):
    np.random.seed(seed)
    _w = jnp.asarray

    def _rec_inputs():
        import jax
        import jax.numpy as jnp
        _gk = jax.random.key(seed)
        x = -0.000202 + 1 * jax.random.normal(jax.random.fold_in(_gk, 1), (100000, 64), jnp.float32)
        src = jax.random.randint(jax.random.fold_in(_gk, 2), (25000,), 0, 100000, jnp.int32)
        dst = jax.random.randint(jax.random.fold_in(_gk, 3), (25000,), 0, 100000, jnp.int32)
        _o = jnp.argsort(dst, stable=True)
        src = src[_o]
        dst = dst[_o]
        edge_attr_32 = 0.000189758 + 1.00013 * jax.random.normal(jax.random.fold_in(_gk, 11), (25000, 32), jnp.float32)
        return (x, src, dst, edge_attr_32)
    x, src, dst, edge_attr_32 = _rec_inputs()

    def _L0_gnn_setup():
        import jax, jax.numpy as jnp
        import numpy as np
        N_NODES = 100000
        N_EDGES = 25000
        NODE_F = 64
        EDGE_F = 32
        BN_EPS = 1e-05
        key = jax.random.key(seed)
        ks = jax.random.split(key, 8)
        in_dim = 2 * NODE_F + EDGE_F
        scale = 1.0 / np.sqrt(in_dim)
        return {'node_attrs': jax.random.normal(ks[0], (N_NODES, NODE_F), jnp.float32), 'edge_index': jax.random.randint(ks[1], (2, N_EDGES), 0, N_NODES, jnp.int64), 'edge_attrs': jax.random.normal(ks[2], (N_EDGES, EDGE_F), jnp.float32), 'W_f': jax.random.normal(ks[3], (in_dim, NODE_F), jnp.float32) * scale, 'b_f': jnp.zeros((NODE_F,), jnp.float32), 'W_s': jax.random.normal(ks[4], (in_dim, NODE_F), jnp.float32) * scale, 'b_s': jnp.zeros((NODE_F,), jnp.float32), 'gamma': jnp.ones((NODE_F,), jnp.float32), 'beta': jnp.zeros((NODE_F,), jnp.float32)}
    _L0_gnn_all = _L0_gnn_setup()
    _L0_gnn_in = {k: v for k, v in _L0_gnn_all.items() if k in ('W_f', 'b_f', 'W_s', 'b_s', 'gamma', 'beta')}
    del _L0_gnn_all
    return {'x': x, 'src': src, 'dst': dst, 'edge_attr_32': edge_attr_32, 'L0_gnn_W_f': _L0_gnn_in['W_f'], 'L0_gnn_b_f': _L0_gnn_in['b_f'], 'L0_gnn_W_s': _L0_gnn_in['W_s'], 'L0_gnn_b_s': _L0_gnn_in['b_s'], 'L0_gnn_gamma': _L0_gnn_in['gamma'], 'L0_gnn_beta': _L0_gnn_in['beta']}

def reference(x, src, dst, edge_attr_32, L0_gnn_W_f, L0_gnn_b_f, L0_gnn_W_s, L0_gnn_b_s, L0_gnn_gamma, L0_gnn_beta):
    import jax
    import jax.numpy as jnp

    def _L0_gnn_ref(node_attrs, edge_index, edge_attrs, W_f, b_f, W_s, b_s, gamma, beta):
        import jax, jax.numpy as jnp
        import numpy as np
        N_NODES = 100000
        N_EDGES = 25000
        NODE_F = 64
        EDGE_F = 32
        BN_EPS = 1e-05
        source, target = (edge_index[0], edge_index[1])
        x_i = node_attrs[source]
        x_j = node_attrs[target]
        z = jnp.concatenate([x_i, x_j, edge_attrs], axis=-1)
        h = jax.nn.sigmoid(z @ W_f + b_f) * jax.nn.softplus(z @ W_s + b_s)
        message = jax.ops.segment_sum(h, source, num_segments=node_attrs.shape[0])
        mean = jnp.mean(message, axis=0)
        var = jnp.mean((message - mean) ** 2, axis=0)
        normed = (message - mean) * jax.lax.rsqrt(var + BN_EPS) * gamma + beta
        return node_attrs + normed
    edge_index = jnp.stack([src, dst])
    h = jnp.maximum(_layernorm(x, axis=-1), 0.0)
    x = x + _L0_gnn_ref(h, edge_index, edge_attr_32, L0_gnn_W_f, L0_gnn_b_f, L0_gnn_W_s, L0_gnn_b_s, L0_gnn_gamma, L0_gnn_beta)
    return x

_drawn_inputs = setup_inputs


def setup_inputs(seed=0):
    import zlib

    import numpy as np

    out = dict(_drawn_inputs(seed))
    spreads = {'L0_gnn_b_f': (0.0, 0.8),
     'L0_gnn_b_s': (0.0, 0.8),
     'L0_gnn_gamma': (1.0, 0.2),
     'L0_gnn_beta': (0.0, 0.1)}
    factors = {}
    for name, (base, spread) in spreads.items():
        noise = np.random.default_rng([zlib.crc32(name.encode()), seed]).standard_normal(out[name].shape)
        drawn = base * np.exp(spread * noise) if base else spread * noise
        out[name] = jnp.asarray(drawn.astype(out[name].dtype))
    for name, factor in factors.items():
        out[name] = (out[name] * factor).astype(out[name].dtype)
    return out
```

```python
from contextlib import ExitStack

import concourse.bass as bass
from concourse import mybir

F32 = mybir.dt.float32
I32 = mybir.dt.int32
ALU = mybir.AluOpType
ACT = mybir.ActivationFunctionType
AX = mybir.AxisListType

P = 128
NODES, EDGES, F, EF = 100000, 25000, 64, 32
EPS = 1e-5
TILES = 4
PAIRS = TILES // 2
GATHERED = 2 * TILES
BULK = 16
ROWS = GATHERED + BULK
E_COLS = EDGES // P
E_REST = EDGES - P * E_COLS
ALL_TILES = E_COLS + 1
GROUPS = ALL_TILES // TILES
LAST = GROUPS - 1
N_ROWS = NODES // P
N_REST = NODES - P * N_ROWS
LAST_ROWS = N_ROWS - BULK * LAST
UNROLL = 6
ITERS = LAST // UNROLL
SLOTS = 3
SPILL = 17
KEPT_ROWS = (GROUPS - SPILL) * BULK
ACC_LAG = 5
DUMP = 3 * P
assert ALL_TILES == TILES * GROUPS and ITERS * UNROLL == LAST and UNROLL % SLOTS == 0
assert 0 < LAST_ROWS < BULK

S_BLK = 68
K_BLK = 64
BLOCKS = [(r, min(S_BLK, SPILL * BULK - r)) for r in range(0, SPILL * BULK, S_BLK)]
SPILLED_BLOCKS = len(BLOCKS)
BLOCKS += [(r, min(K_BLK, N_ROWS - r)) for r in range(SPILL * BULK, N_ROWS, K_BLK)]
NB = len(BLOCKS)
M_BUFS = 4
SQ_ROWS = 16
SQ_BUFS = 3


class Group:

    def __init__(self, it, off):
        self.it, self.off = it, off

    def back(self, n):
        return Group(self.it, self.off - n)

    @property
    def known(self):
        return isinstance(self.it, int)

    @property
    def n(self):
        return self.it * UNROLL + self.off

    def slot(self, ring):
        return self.off % ring

    def uses(self, ring):
        return self.it * (UNROLL // ring) + self.off // ring

    def exists(self):
        return not self.known or 0 <= self.n < GROUPS


def wait_group(eng, sem, g, per=1):
    if not g.known or g.n >= 0:
        eng.wait_ge(sem, per * (g.n + 1) if per > 1 else g.n + 1)


def run_groups(eng, step, extra):
    for u in range(UNROLL):
        step(Group(0, u))
    with eng.Fori(1, ITERS) as it:
        for u in range(UNROLL):
            step(Group(it, u))
    for u in range(1 + extra):
        step(Group(ITERS, u))


def build(nc, x, src, dst, ea, w_f, b_f, w_s, b_s, gamma, beta, out, msgs, y_spill):
    x_rows = x[0:P * N_ROWS, :].rearrange("(p r) f -> p r f", p=P)
    ea_tiles = ea[0:P * E_COLS, :].rearrange("(p t) f -> p t f", p=P)
    m_rows = msgs[0:P * N_ROWS, :].rearrange("(p r) f -> p r f", p=P)
    out_rows = out[0:P * N_ROWS, :].rearrange("(p r) f -> p r f", p=P)

    with ExitStack() as outer:
        def sem(name):
            return outer.enter_context(nc.semaphore(name))

        def keep(name, shape, dt=F32):
            return outer.enter_context(nc.sbuf_tensor(name, shape, dt))

        y_kept = keep("y_kept", [P, KEPT_ROWS, F])
        ones = keep("ones", [P, P])
        eps_col = keep("eps_col", [P, 1])
        one_col = keep("one_col", [P, 1])
        msg_sum = keep("msg_sum", [P, F])

        stage_one(nc, sem, x, src, dst, ea, w_f, b_f, w_s, b_s, msgs, y_spill,
                  x_rows, ea_tiles, m_rows, y_kept, ones, eps_col, one_col, msg_sum)
        stage_two(nc, sem, msgs, y_spill, gamma, beta, out, m_rows, out_rows,
                  y_kept, ones, eps_col, msg_sum)


def stage_one(nc, sem, x, src, dst, ea, w_f, b_f, w_s, b_s, msgs, y_spill,
              x_rows, ea_tiles, m_rows, y_kept, ones, eps_col, one_col, msg_sum):
    with ExitStack() as ctx:
        def sb(name, shape, dt=F32):
            return ctx.enter_context(nc.sbuf_tensor(name, shape, dt))

        def ps(name, shape):
            return ctx.enter_context(nc.psum_tensor(name, shape, F32))

        ids = sb("ids", [P, 2, ALL_TILES], I32)
        src_f = sb("src_f", [P, ALL_TILES])
        dump_row = sb("dump_row", [P, TILES])
        small = sb("small", [P, 4])
        real = sb("real", [P, P])
        ident = sb("ident", [P, P])
        earlier = sb("earlier", [P, P])
        zeros = sb("zeros", [P, BULK * F])
        w_z = sb("w_z", [P, 2 * F])
        w_e = sb("w_e", [P, TILES, 2 * F])
        b_row = sb("b_row", [1, TILES, 2 * F])
        own = sb("own", [P, UNROLL, TILES])
        gidx = sb("gidx", [P, UNROLL, 2, TILES], I32)
        xg = sb("xg", [P, SLOTS, ROWS, F])
        eas = sb("eas", [P, SLOTS, TILES, EF])
        xc = sb("xc", [P, 2, ROWS, F])
        sq = sb("sq", [P, ROWS, F])
        row_sum = sb("row_sum", [P, ROWS])
        row_ssq = sb("row_ssq", [P, ROWS])
        row_lnv = sb("row_lnv", [P, ROWS])
        row_rstd = sb("row_rstd", [P, ROWS])
        z_t = sb("z_t", [P, TILES, P])
        ea_t = sb("ea_t", [P, P])
        spl = sb("spl", [P, TILES, 2 * F])
        soft = sb("soft", [P, TILES, 2 * F])
        gate = sb("gate", [P, TILES, F])
        msg = sb("msg", [P, TILES, F])
        same = sb("same", [P, PAIRS, 2, 2 * P])
        before = sb("before", [P, PAIRS, 2, P])
        gap = sb("gap", [P, TILES])
        moved = sb("moved", [P, TILES])
        target = sb("target", [P, UNROLL, TILES], I32)
        comb = sb("comb", [P, UNROLL, TILES, F])

        ps_z = ps("ps_z", [P, TILES, P])
        ps_e = ps("ps_e", [P, P])
        ps_v = ps("ps_v", [P, TILES, 2 * F])
        ps_src = ps("ps_src", [P, TILES, P])
        ps_c = ps("ps_c", [P, TILES, F])
        ps_n = ps("ps_n", [P, TILES])
        ps_sum = ps("ps_sum", [P, F])

        ids_loaded = sem("ids_loaded")
        w_loaded = sem("w_loaded")
        w_cleared = sem("w_cleared")
        masks_set = sem("masks_set")
        masks_made = sem("masks_made")
        consts = sem("consts")
        prep = sem("prep")
        zeros_set = sem("zeros_set")
        table_zeroed = sem("table_zeroed")
        loaded = [sem(f"loaded{i}") for i in range(SLOTS)]
        gathered = [sem(f"gathered{i}") for i in range(SLOTS)]
        staged = sem("staged")
        gathers_begun = sem("gathers_begun")
        own_staged = sem("own_staged")
        summed = sem("summed")
        centred = sem("centred")
        squared = sem("squared")
        ssq_done = sem("ssq_done")
        lnv_done = sem("lnv_done")
        rstd_done = sem("rstd_done")
        h_done = sem("h_done")
        y_done = sem("y_done")
        spilled = sem("spilled")
        ea_turned = sem("ea_turned")
        ea_copied = sem("ea_copied")
        z_turned = sem("z_turned")
        z_copied = sem("z_copied")
        v_done = sem("v_done")
        spl_steps = sem("spl_steps")
        spl_done = sem("spl_done")
        soft_done = sem("soft_done")
        gate_done = sem("gate_done")
        msg_done = sem("msg_done")
        src_spread = sem("src_spread")
        same_done = sem("same_done")
        before_done = sem("before_done")
        comb_done = sem("comb_done")
        comb_copied = sem("comb_copied")
        gap_done = sem("gap_done")
        moved_done = sem("moved_done")
        target_done = sem("target_done")
        accumulated = sem("accumulated")
        slots_free = sem("slots_free")
        sum_started = sem("sum_started")
        sum_kept = sem("sum_kept")

        LOADS = 2
        LAST_LOADS = 5

        block = ctx.enter_context(nc.Block())

        @block.sync
        def _(sp):
            for c, v in enumerate((src, dst)):
                sp.dma_start(ids[:, c, 0:E_COLS],
                             v[0:P * E_COLS].rearrange("(p t) -> p t", p=P)).then_inc(ids_loaded, 16)
                sp.dma_start(ids[0:E_REST, c, E_COLS:ALL_TILES],
                             v[P * E_COLS:EDGES].rearrange("(p t) -> p t", t=1)).then_inc(ids_loaded, 16)
                sp.dma_start(ids[E_REST:P, c, E_COLS:ALL_TILES],
                             v[0:P - E_REST].rearrange("(p t) -> p t", t=1)).then_inc(ids_loaded, 16)

            def load(g):
                s = g.slot(SLOTS)
                wait_group(sp, y_done, g.back(SLOTS))
                wait_group(sp, ea_turned, g.back(SLOTS))
                if g.known and g.n == LAST:
                    sp.dma_start(xg[:, s, GATHERED:GATHERED + LAST_ROWS, :],
                                 x_rows[:, BULK * LAST:N_ROWS, :]).then_inc(loaded[s], 16)
                    sp.dma_start(xg[0:N_REST, s, GATHERED + LAST_ROWS, :],
                                 x[P * N_ROWS:NODES, :]).then_inc(loaded[s], 16)
                    sp.dma_start(eas[:, s, 0:TILES - 1, :],
                                 ea_tiles[:, E_COLS - TILES + 1:E_COLS, :]).then_inc(loaded[s], 16)
                    sp.dma_start(eas[0:E_REST, s, TILES - 1, :],
                                 ea[P * E_COLS:EDGES, :]).then_inc(loaded[s], 16)
                    sp.dma_start(eas[E_REST:P, s, TILES - 1, :],
                                 ea[0:P - E_REST, :]).then_inc(loaded[s], 16)
                elif not g.known or g.n < LAST:
                    sp.dma_start(xg[:, s, GATHERED:ROWS, :],
                                 x_rows[:, bass.ds(g.n * BULK, BULK), :]).then_inc(loaded[s], 16)
                    sp.dma_start(eas[:, s, :, :],
                                 ea_tiles[:, bass.ds(g.n * TILES, TILES), :]).then_inc(loaded[s], 16)

            run_groups(sp, load, 0)

        @block.gpsimd
        def _(pool):
            pool.sem_inc(slots_free, PAIRS * UNROLL - 1)
            pool.memset(ident[:, :], 0.0).then_inc(masks_set, 1)
            pool.memset(earlier[:, :], 1.0).then_inc(masks_set, 1)
            pool.wait_ge(masks_set, 2)
            pool.affine_select(out=ident[:, :], in_=ident[:, :], compare_op=ALU.not_equal, fill=1.0,
                               base=0, pattern=[[-1, P]], channel_multiplier=1).then_inc(masks_made, 1)
            pool.affine_select(out=earlier[:, :], in_=earlier[:, :], compare_op=ALU.is_gt, fill=0.0,
                               base=0, pattern=[[1, P]], channel_multiplier=-1).then_inc(masks_made, 1)

            def gather(g, q):
                s = g.slot(SLOTS)
                for j in (2 * q, 2 * q + 1):
                    for c in range(2):
                        pool.indirect_dma_start(
                            xg[:, s, 2 * j + c, :], None, x,
                            bass.IndirectOffsetOnAxis(ap=gidx[:, g.slot(UNROLL), c, j:j + 1], axis=0),
                        ).then_inc(gathered[s], 16)

            def accumulate(g, q):
                if g.known:
                    pairs = g.n * PAIRS + q
                    if pairs:
                        pool.wait_ge(accumulated, 32 * pairs)
                else:
                    pool.wait_ge(accumulated, 32 * PAIRS * g.n + 32 * q)
                pool.sem_inc(slots_free, 1)
                for j in (2 * q, 2 * q + 1):
                    pool.indirect_dma_start(
                        msgs, bass.IndirectOffsetOnAxis(ap=target[:, g.slot(UNROLL), j:j + 1], axis=0),
                        comb[:, g.slot(UNROLL), j, :], None, compute_op=ALU.add,
                    ).then_inc(accumulated, 16)

            def step(g):
                old = g.back(ACC_LAG)
                if g.known and g.n == ACC_LAG:
                    pool.wait_ge(table_zeroed, 16 * 3)
                if not g.known or g.n < GROUPS:
                    wait_group(pool, staged, g)
                    wait_group(pool, centred, g.back(SLOTS))
                    pool.sem_inc(gathers_begun, 1)
                    gather(g, 0)
                if old.exists():
                    wait_group(pool, comb_copied, old)
                    wait_group(pool, target_done, old)
                    accumulate(old, 0)
                if not g.known or g.n < GROUPS:
                    gather(g, 1)
                if old.exists():
                    accumulate(old, 1)

            for u in range(UNROLL):
                step(Group(0, u))
            with pool.Fori(1, ITERS) as it:
                for u in range(UNROLL):
                    step(Group(it, u))
            for u in range(1 + ACC_LAG):
                step(Group(ITERS, u))
            pool.wait_ge(accumulated, 16 * ALL_TILES)

        @block.vector
        def _(dve):
            dve.memset(zeros[:, :], 0.0).then_inc(zeros_set, 1)
            dve.memset(w_e[:, :, :], 0.0).then_inc(w_cleared, 1)
            dve.memset(ones[:, :], 1.0)
            dve.memset(one_col[:, :], 1.0)
            dve.memset(eps_col[:, :], EPS).then_inc(consts, 1)
            dve.wait_ge(masks_made, 2)
            dve.tensor_reduce(small[:, 0:1], earlier[:, :], AX.X, ALU.add).then_inc(prep, 1)
            dve.wait_ge(prep, 1)
            for j in range(TILES):
                dve.tensor_scalar(dump_row[:, j:j + 1], small[:, 0:1], float(NODES + P * (j % 2)), None, ALU.add)
            dve.tensor_scalar(small[:, 1:2], small[:, 0:1], float(P - 1 - E_REST) + 0.5, None, ALU.is_gt)
            dve.tensor_scalar(small[:, 2:3], small[:, 0:1], float(NODES + 2 * P), None, ALU.add)
            dve.wait_ge(ids_loaded, 96)
            dve.tensor_copy(src_f[:, :], ids[:, 0, :]).then_inc(prep, 1)
            dve.wait_ge(prep, 2)
            dve.tensor_scalar(real[:, :], ones[:, :], small[:, 1:2], None, ALU.mult)
            dve.tensor_tensor(small[:, 3:4], src_f[:, E_COLS:ALL_TILES], small[:, 2:3],
                              ALU.subtract).then_inc(prep, 1)
            dve.wait_ge(prep, 3)
            dve.tensor_scalar(src_f[:, E_COLS:ALL_TILES], small[:, 3:4], small[:, 1:2], small[:, 2:3],
                              ALU.mult, ALU.add).then_inc(prep, 1)
            dve.wait_ge(w_loaded, 16 * (4 + 2 * TILES + 2 * TILES))
            dve.tensor_scalar(w_z[:, 0:F], w_z[:, 0:F], -1.0, None, ALU.mult)
            dve.tensor_scalar(w_e[:, :, 0:F], w_e[:, :, 0:F], -1.0, None, ALU.mult)
            dve.tensor_scalar(b_row[:, :, 0:F], b_row[:, :, 0:F], -1.0, None, ALU.mult).then_inc(prep, 1)
            dve.tensor_copy(gidx[:, 0, :, :], ids[:, :, 0:TILES]).then_inc(staged, 1)
            dve.wait_ge(prep, 4)
            dve.tensor_copy(own[:, 0, :], src_f[:, 0:TILES]).then_inc(own_staged, 1)

            def stage_indices(g):
                dve.tensor_copy(gidx[:, g.slot(UNROLL), :, :],
                                ids[:, :, bass.ds(g.n * TILES, TILES)]).then_inc(staged, 1)
                wait_group(dve, target_done, g.back(UNROLL))
                dve.tensor_copy(own[:, g.slot(UNROLL), :],
                                src_f[:, bass.ds(g.n * TILES, TILES)]).then_inc(own_staged, 1)

            def sums(g):
                s = g.slot(SLOTS)
                dve.wait_ge(gathered[s], 16 * GATHERED * g.uses(SLOTS) + 16 * GATHERED)
                extra = 16 * (LAST_LOADS - LOADS) if g.known and g.n == LAST else 0
                dve.wait_ge(loaded[s], 16 * LOADS * g.uses(SLOTS) + 16 * LOADS + extra)
                wait_group(dve, centred, g.back(1))
                dve.tensor_reduce(row_sum[:, :], xg[:, s, :, :], AX.X, ALU.add).then_inc(summed, 1)

            def centre(g):
                wait_group(dve, summed, g)
                wait_group(dve, z_turned, g.back(2))
                wait_group(dve, y_done, g.back(2))
                dve.scalar_tensor_tensor(
                    out=xc[:, g.slot(2), :, :], in0=row_sum[:, :].unsqueeze(2).to_broadcast([P, ROWS, F]),
                    scalar=-1.0 / F, in1=xg[:, g.slot(SLOTS), :, :], op0=ALU.mult, op1=ALU.add,
                ).then_inc(centred, 1)

            def sum_squares(g):
                wait_group(dve, squared, g)
                wait_group(dve, lnv_done, g.back(1))
                dve.tensor_reduce(row_ssq[:, :], sq[:, :, :], AX.X, ALU.add).then_inc(ssq_done, 1)

            def same_source(g):
                wait_group(dve, src_spread, g)
                wait_group(dve, comb_done, g.back(1))
                cols = own[:, g.slot(UNROLL), :].rearrange("p (q b) -> p q b", q=PAIRS)
                for q in range(PAIRS):
                    ins = dve.tensor_tensor(
                        same[:, q, :, :],
                        ps_src[:, 2 * q:2 * q + 2, :].rearrange("p a i -> p (a i)").unsqueeze(1)
                        .to_broadcast([P, 2, 2 * P]),
                        cols[:, q, :].unsqueeze(2).to_broadcast([P, 2, 2 * P]), ALU.is_equal)
                ins.then_inc(same_done, 1)
                wait_group(dve, same_done, g)
                for a in range(2):
                    ins = dve.tensor_tensor(before[:, :, a, :], same[:, :, a, a * P:(a + 1) * P],
                                            earlier[:, :].unsqueeze(1).to_broadcast([P, PAIRS, P]), ALU.mult)
                ins.then_inc(before_done, 1)

            def targets(g):
                wait_group(dve, comb_done, g)
                rows = own[:, g.slot(UNROLL), :]
                wait_group(dve, moved_done, g.back(1))
                dve.tensor_tensor(gap[:, :], dump_row[:, :], rows, ALU.subtract).then_inc(gap_done, 1)
                wait_group(dve, gap_done, g)
                wait_group(dve, target_done, g.back(1))
                dve.scalar_tensor_tensor(out=moved[:, :], in0=ps_n[:, :], scalar=0.0, in1=gap[:, :],
                                         op0=ALU.is_gt, op1=ALU.mult).then_inc(moved_done, 1)
                wait_group(dve, moved_done, g)
                wait_group(dve, slots_free, g, PAIRS)
                dve.tensor_tensor(target[:, g.slot(UNROLL), :], moved[:, :], rows, ALU.add).then_inc(target_done, 1)

            def softplus(g):
                wait_group(dve, spl_done, g)
                wait_group(dve, msg_done, g.back(1))
                wait_group(dve, gate_done, g.back(1))
                dve.scalar_tensor_tensor(out=soft[:, :, :], in0=ps_v[:, :, :], scalar=0.0, in1=spl[:, :, :],
                                         op0=ALU.max, op1=ALU.add).then_inc(soft_done, 1)

            def normalise(g):
                wait_group(dve, rstd_done, g)
                h = xc[:, g.slot(2), :, :]
                dve.scalar_tensor_tensor(out=h, in0=h, scalar=0.0,
                                         in1=row_rstd[:, :].unsqueeze(2).to_broadcast([P, ROWS, F]),
                                         op0=ALU.max, op1=ALU.mult).then_inc(h_done, 1)

            def residual(g, spill):
                wait_group(dve, h_done, g)
                if not spill:
                    dve.wait_ge(spilled, 16 * SPILL)
                row = g.n * BULK - (0 if spill else SPILL * BULK)
                dve.tensor_tensor(y_kept[:, bass.ds(row, BULK), :], xc[:, g.slot(2), GATHERED:ROWS, :],
                                  xg[:, g.slot(SLOTS), GATHERED:ROWS, :], ALU.add).then_inc(y_done, 1)

            def message(g):
                wait_group(dve, gate_done, g)
                wait_group(dve, comb_done, g.back(1))
                dve.tensor_tensor(msg[:, :, :], gate[:, :, :], soft[:, :, F:2 * F], ALU.mult).then_inc(msg_done, 1)

            def step(g, spill):
                now = not g.known or g.n < GROUPS
                if now and not (g.known and g.n == LAST):
                    stage_indices(g.back(-1))
                if now:
                    sums(g)
                    centre(g)
                if g.back(3).exists():
                    targets(g.back(3))
                if g.back(1).exists():
                    sum_squares(g.back(1))
                if g.back(2).exists():
                    same_source(g.back(2))
                    softplus(g.back(2))
                if g.back(1).exists():
                    normalise(g.back(1))
                    residual(g.back(1), spill)
                if g.back(2).exists():
                    message(g.back(2))

            for u in range(UNROLL):
                step(Group(0, u), True)
            first_kept = (SPILL + 1) // UNROLL
            with dve.Fori(1, first_kept) as it:
                for u in range(UNROLL):
                    step(Group(it, u), True)
            with dve.Fori(first_kept, ITERS) as it:
                for u in range(UNROLL):
                    step(Group(it, u), False)
            for u in range(4):
                step(Group(ITERS, u), False)

        @block.scalar
        def _(act):
            act.wait_ge(zeros_set, 1)
            whole = N_ROWS // BULK * BULK
            act.dma_start(m_rows[:, 0:whole, :].rearrange("p (n r) f -> p n (r f)", r=BULK),
                          zeros[:, :].unsqueeze(1).to_broadcast([P, whole // BULK, BULK * F])).then_inc(table_zeroed, 16)
            act.dma_start(m_rows[:, whole:N_ROWS, :],
                          zeros[:, 0:(N_ROWS - whole) * F].rearrange("p (r f) -> p r f", f=F)).then_inc(table_zeroed, 16)
            rest = (N_REST + DUMP) // 32
            act.dma_start(msgs[P * N_ROWS:NODES + DUMP, :].rearrange("(p r) f -> p (r f)", p=32),
                          zeros[0:32, 0:rest * F]).then_inc(table_zeroed, 16)
            act.wait_ge(w_cleared, 1)
            for c, (w, b) in enumerate(((w_f, b_f), (w_s, b_s))):
                cols = slice(c * F, (c + 1) * F)
                act.dma_start(w_z[0:F, cols], w[0:F, :]).then_inc(w_loaded, 16)
                act.dma_start(w_z[F:2 * F, cols], w[F:2 * F, :]).then_inc(w_loaded, 16)
                for j in range(TILES):
                    act.dma_start(w_e[j * EF:(j + 1) * EF, j, cols], w[2 * F:2 * F + EF, :]).then_inc(w_loaded, 16)
                    act.dma_start(b_row[0:1, j, cols], b.rearrange("(a f) -> a f", a=1)).then_inc(w_loaded, 16)
            act.wait_ge(consts, 1)

            def square(g):
                wait_group(act, centred, g)
                wait_group(act, ssq_done, g.back(1))
                act.activation(sq[:, :, :], xc[:, g.slot(2), :, :], ACT.Square).then_inc(squared, 1)

            def rstd(g):
                wait_group(act, ssq_done, g)
                wait_group(act, rstd_done, g.back(1))
                act.activation(row_lnv[:, :], row_ssq[:, :], ACT.Ln, bias=eps_col[:, 0:1],
                               scale=1.0 / F).then_inc(lnv_done, 1)
                wait_group(act, lnv_done, g)
                wait_group(act, h_done, g.back(1))
                act.activation(row_rstd[:, :], row_lnv[:, :], ACT.Exp, scale=-0.5).then_inc(rstd_done, 1)

            def gates(g):
                wait_group(act, soft_done, g)
                wait_group(act, msg_done, g.back(1))
                act.activation(gate[:, :, :], soft[:, :, 0:F], ACT.Exp, scale=-1.0).then_inc(gate_done, 1)

            def copy_turned(g):
                wait_group(act, ea_turned, g)
                wait_group(act, v_done, g.back(1))
                act.activation(ea_t[:, :], ps_e[:, :], ACT.Copy).then_inc(ea_copied, 1)
                wait_group(act, z_turned, g)
                act.activation(z_t[:, :, :], ps_z[:, :, :], ACT.Copy).then_inc(z_copied, 1)

            def softplus_log(g):
                wait_group(act, v_done, g)
                wait_group(act, soft_done, g.back(1))
                act.activation(spl[:, :, :], ps_v[:, :, :], ACT.Abs).then_inc(spl_steps, 1)
                act.wait_ge(spl_steps, 2 * g.n + 1)
                act.activation(spl[:, :, :], spl[:, :, :], ACT.Exp, scale=-1.0).then_inc(spl_steps, 1)
                act.wait_ge(spl_steps, 2 * g.n + 2)
                act.activation(spl[:, :, :], spl[:, :, :], ACT.Ln, bias=one_col[:, 0:1]).then_inc(spl_done, 1)

            def copy_comb(g):
                wait_group(act, comb_done, g)
                wait_group(act, slots_free, g, PAIRS)
                act.activation(comb[:, g.slot(UNROLL), :, :], ps_c[:, :, :], ACT.Copy).then_inc(comb_copied, 1)

            def spill(g):
                wait_group(act, y_done, g)
                act.dma_start(y_spill[:, bass.ds(g.n * BULK, BULK), :],
                              y_kept[:, bass.ds(g.n * BULK, BULK), :]).then_inc(spilled, 16)

            def step(g, spills):
                if not g.known or g.n < GROUPS:
                    square(g)
                if g.back(1).exists():
                    rstd(g.back(1))
                if g.back(2).exists():
                    gates(g.back(2))
                if g.back(1).exists():
                    copy_turned(g.back(1))
                    softplus_log(g.back(1))
                if g.back(2).exists():
                    copy_comb(g.back(2))
                if spills and g.back(1).exists():
                    spill(g.back(1))

            for u in range(UNROLL):
                step(Group(0, u), True)
            first_kept = (SPILL + 1) // UNROLL
            with act.Fori(1, first_kept) as it:
                for u in range(UNROLL):
                    step(Group(it, u), True)
            with act.Fori(first_kept, ITERS) as it:
                for u in range(UNROLL):
                    step(Group(it, u), False)
            for u in range(3):
                step(Group(ITERS, u), False)
            act.activation(msg_sum[:, :], ps_sum[:, :], ACT.Copy).then_inc(sum_kept, 1)
            act.wait_ge(spilled, 16 * SPILL)

        @block.tensor
        def _(pe):
            pe.wait_ge(masks_made, 2)
            pe.wait_ge(consts, 1)
            pe.wait_ge(prep, 5)
            pe.matmul(ps_sum[:, :], zeros[:, 0:P], zeros[:, 0:F], start=True, stop=True,
                      skip_group_check=True).then_inc(sum_started, 1)

            def turn_edges(g):
                extra = 16 * (LAST_LOADS - LOADS) if g.known and g.n == LAST else 0
                pe.wait_ge(loaded[g.slot(SLOTS)], 16 * LOADS * g.uses(SLOTS) + 16 * LOADS + extra)
                wait_group(pe, ea_copied, g.back(1))
                pe.transpose(ps_e[:, :], eas[:, g.slot(SLOTS), :, :].rearrange("p t f -> p (t f)"),
                             ident[:, :]).then_inc(ea_turned, 1)

            def spread_sources(g):
                wait_group(pe, same_done, g.back(1))
                wait_group(pe, own_staged, g)
                for j in range(TILES):
                    ins = pe.matmul(ps_src[:, j, :], own[:, g.slot(UNROLL), j:j + 1].to_broadcast([P, P]),
                                    ident[:, :], start=True, stop=True)
                ins.then_inc(src_spread, 1)

            def turn_z(g):
                wait_group(pe, h_done, g)
                wait_group(pe, z_copied, g.back(1))
                for j in range(TILES):
                    ins = pe.transpose(ps_z[:, j, :],
                                       xc[:, g.slot(2), 2 * j:2 * j + 2, :].rearrange("p c f -> p (c f)"),
                                       ident[:, :])
                ins.then_inc(z_turned, 1)

            def products(g):
                wait_group(pe, soft_done, g.back(1))
                wait_group(pe, ea_copied, g)
                wait_group(pe, z_copied, g)
                pe.matmul(ps_v[:, :, :].rearrange("p t f -> p (t f)"), ones[0:1, :],
                          b_row[0:1, :, :].rearrange("p t f -> p (t f)"), start=True, stop=True)
                for j in range(TILES):
                    pe.matmul(ps_v[:, j, :], ea_t[:, :], w_e[:, j, :], start=False, stop=True,
                              skip_group_check=True)
                    ins = pe.matmul(ps_v[:, j, :], z_t[:, j, :], w_z[:, :], start=False, stop=True,
                                    skip_group_check=True)
                ins.then_inc(v_done, 1)

            def combine(g):
                wait_group(pe, before_done, g)
                wait_group(pe, msg_done, g)
                wait_group(pe, comb_copied, g.back(1))
                wait_group(pe, moved_done, g.back(1))
                for q in range(PAIRS):
                    for a in range(2):
                        j = 2 * q + a
                        for b in range(2):
                            pe.matmul(ps_c[:, j, :], same[:, q, b, a * P:(a + 1) * P], msg[:, 2 * q + b, :],
                                      start=(b == 0), stop=(b == 1))
                        if a == 1:
                            pe.matmul(ps_n[:, j:j + 1], same[:, q, 0, P:2 * P], ones[:, 0:1],
                                      start=True, stop=False)
                        pe.matmul(ps_n[:, j:j + 1], before[:, q, a, :], ones[:, 0:1],
                                  start=(a == 0), stop=True)
                last = g.known and g.n == LAST
                for j in range(TILES):
                    w = real if last and j == TILES - 1 else ones
                    ins = pe.matmul(ps_sum[:, :], w[:, :], msg[:, j, :], start=False, stop=True, skip_group_check=True)
                ins.then_inc(comb_done, 1)

            def step(g):
                if g.back(1).exists():
                    turn_edges(g.back(1))
                    spread_sources(g.back(1))
                    turn_z(g.back(1))
                    products(g.back(1))
                if g.back(2).exists():
                    combine(g.back(2))

            run_groups(pe, step, 2)


def stage_two(nc, sem, msgs, y_spill, gamma, beta, out, m_rows, out_rows, y_kept, ones, eps_col, msg_sum):
    with ExitStack() as ctx:
        def sb(name, shape, dt=F32):
            return ctx.enter_context(nc.sbuf_tensor(name, shape, dt))

        m_buf = sb("m_buf", [P, M_BUFS, max(n for _, n in BLOCKS), F])
        m_rest = sb("m_rest", [N_REST, F])
        sq_acc = sb("sq_acc", [P, SQ_ROWS, F])
        sq_row = sb("sq_row", [P, F])
        gam = sb("gam", [P, F])
        bet = sb("bet", [P, F])
        mean = sb("mean", [P, F])
        mean2 = sb("mean2", [P, F])
        var = sb("var", [P, F])
        lnv = sb("lnv", [P, F])
        scale = sb("scale", [P, F])
        shift = sb("shift", [P, F])
        ps_sq = [ctx.enter_context(nc.psum_tensor(f"ps_sq{i}", [P, SQ_ROWS, F], F32)) for i in range(SQ_BUFS)]
        ps_tot = ctx.enter_context(nc.psum_tensor("ps_tot", [P, F], F32))

        m_loaded = [sem(f"m_loaded{i}") for i in range(M_BUFS)]
        rest_loaded = sem("rest_loaded")
        affine_loaded = sem("affine_loaded")
        y_loaded = [sem(f"y_loaded{i}") for i in range(SPILLED_BLOCKS)]
        block_squared = sem("block_squared")
        part_squared = sem("part_squared")
        part_cleared = sem("part_cleared")
        part_added = sem("part_added")
        acc_reduced = sem("acc_reduced")
        total_ready = sem("total_ready")
        var_ready = sem("var_ready")
        ln_ready = sem("ln_ready")
        rstd_ready = sem("rstd_ready")
        chain = sem("chain")
        shift_ready = sem("shift_ready")
        scaled = sem("scaled")
        y_added = sem("y_added")
        shifted = sem("shifted")
        rest_done = sem("rest_done")
        stored = [sem(f"stored{i}") for i in range(M_BUFS)]
        rest_stored = sem("rest_stored")

        parts = [(b, r, min(SQ_ROWS, n - r)) for b, (_, n) in enumerate(BLOCKS) for r in range(0, n, SQ_ROWS)]
        held = list(range(NB - M_BUFS, NB))
        order = held + list(range(SPILLED_BLOCKS, NB - M_BUFS)) + list(range(SPILLED_BLOCKS))
        assert len(order) == NB and SPILLED_BLOCKS <= M_BUFS
        rest_row = (LAST - SPILL) * BULK + LAST_ROWS

        def buf_of(i):
            return order[i] % M_BUFS if i < M_BUFS else order[i % M_BUFS] % M_BUFS

        def loads_of(i):
            b = buf_of(i)
            return len([k for k in range(NB) if k % M_BUFS == b]) + len(
                [k for k in range(M_BUFS, i + 1) if buf_of(k) == b])

        def stores_of(i):
            return len([k for k in range(i + 1) if buf_of(k) == buf_of(i)])

        def y_of(b):
            r0, n = BLOCKS[b]
            if b >= SPILLED_BLOCKS:
                return y_kept[:, r0 - SPILL * BULK:r0 - SPILL * BULK + n, :]
            return y_kept[:, b * S_BLK:b * S_BLK + n, :]

        takes = {}
        for b in range(SPILLED_BLOCKS):
            lo, hi = b * S_BLK, b * S_BLK + BLOCKS[b][1]
            over = [i for i, k in enumerate(order) if k >= SPILLED_BLOCKS
                    and BLOCKS[k][0] - SPILL * BULK < hi and BLOCKS[k][0] - SPILL * BULK + BLOCKS[k][1] > lo]
            takes[b] = max(over)

        block = ctx.enter_context(nc.Block())

        @block.sync
        def _(sp):
            for b, (r0, n) in enumerate(BLOCKS):
                if b >= M_BUFS:
                    sp.wait_ge(block_squared, b - M_BUFS + 1)
                sp.dma_start(m_buf[:, b % M_BUFS, 0:n, :], m_rows[:, r0:r0 + n, :]).then_inc(m_loaded[b % M_BUFS], 16)
            sp.dma_start(m_rest[:, :], msgs[P * N_ROWS:NODES, :]).then_inc(rest_loaded, 16)
            sp.dma_start(gam[:, :], gamma.rearrange("(a f) -> a f", a=1).to_broadcast([P, F])).then_inc(affine_loaded, 16)
            sp.dma_start(bet[:, :], beta.rearrange("(a f) -> a f", a=1).to_broadcast([P, F])).then_inc(affine_loaded, 16)
            for i in range(M_BUFS, NB):
                b = order[i]
                r0, n = BLOCKS[b]
                if b < SPILLED_BLOCKS:
                    sp.wait_ge(y_added, takes[b] + 1)
                    sp.dma_start(y_of(b), y_spill[:, r0:r0 + n, :]).then_inc(y_loaded[b], 16)
                sp.wait_ge(stored[buf_of(i)], 16 * stores_of(i - M_BUFS))
                sp.dma_start(m_buf[:, buf_of(i), 0:n, :], m_rows[:, r0:r0 + n, :]).then_inc(m_loaded[buf_of(i)], 16)

        @block.scalar
        def _(act):
            for k, (b, r, n) in enumerate(parts):
                if r == 0:
                    act.wait_ge(m_loaded[b % M_BUFS], 16 * (b // M_BUFS + 1))
                if k >= SQ_BUFS:
                    act.wait_ge(part_added, k - SQ_BUFS + 1)
                ins = act.activation(ps_sq[k % SQ_BUFS][:, 0:n, :], m_buf[:, b % M_BUFS, r:r + n, :], ACT.Square)
                ins.then_inc(part_squared, 1)
                if r + n == BLOCKS[b][1]:
                    act.wait_ge(part_squared, k + 1)
                    act.sem_inc(block_squared, 1)
            act.wait_ge(rest_loaded, 16)
            act.wait_ge(part_added, len(parts) - SQ_BUFS + 1)
            act.activation(ps_sq[len(parts) % SQ_BUFS][0:N_REST, 0, :], m_rest[:, :], ACT.Square).then_inc(part_squared, 1)
            act.wait_ge(var_ready, 1)
            act.activation(lnv[:, :], var[:, :], ACT.Ln, bias=eps_col[:, 0:1]).then_inc(ln_ready, 1)
            act.wait_ge(ln_ready, 1)
            act.activation(var[:, :], lnv[:, :], ACT.Exp, scale=-0.5).then_inc(rstd_ready, 1)
            for i, b in enumerate(order):
                r0, n = BLOCKS[b]
                act.wait_ge(shifted, i + 1)
                act.dma_start(out_rows[:, r0:r0 + n, :], m_buf[:, buf_of(i), 0:n, :]).then_inc(stored[buf_of(i)], 16)
            act.wait_ge(rest_done, 3)
            act.dma_start(out[P * N_ROWS:NODES, :], m_rest[:, :]).then_inc(rest_stored, 16)
            for k in range(M_BUFS):
                last = max(i for i in range(NB) if buf_of(i) == k)
                act.wait_ge(stored[k], 16 * stores_of(last))
            act.wait_ge(rest_stored, 16)

        @block.tensor
        def _(pe):
            pe.wait_ge(acc_reduced, 1)
            pe.matmul(ps_tot[:, :], ones[:, :], sq_row[:, :], start=True, stop=True).then_inc(total_ready, 1)

        @block.vector
        def _(dve):
            dve.memset(sq_acc[:, :, :], 0.0).then_inc(part_cleared, 1)
            dve.wait_ge(part_cleared, 1)
            for k, (b, r, n) in enumerate(parts):
                dve.wait_ge(part_squared, k + 1)
                if k:
                    dve.wait_ge(part_added, k)
                dve.tensor_tensor(sq_acc[:, 0:n, :], sq_acc[:, 0:n, :], ps_sq[k % SQ_BUFS][:, 0:n, :],
                                  ALU.add).then_inc(part_added, 1)
            k = len(parts)
            dve.wait_ge(part_squared, k + 1)
            dve.wait_ge(part_added, k)
            dve.tensor_tensor(sq_acc[0:N_REST, 0, :], sq_acc[0:N_REST, 0, :], ps_sq[k % SQ_BUFS][0:N_REST, 0, :],
                              ALU.add).then_inc(part_added, 1)
            dve.wait_ge(part_added, k + 1)
            dve.tensor_reduce(sq_row[:, :], sq_acc[:, :, :].rearrange("p r f -> p f r"), AX.X,
                              ALU.add).then_inc(acc_reduced, 1)
            dve.tensor_scalar(mean[:, :], msg_sum[:, :], 1.0 / NODES, None, ALU.mult).then_inc(chain, 1)
            dve.wait_ge(chain, 1)
            dve.tensor_tensor(mean2[:, :], mean[:, :], mean[:, :], ALU.mult).then_inc(chain, 1)
            dve.wait_ge(chain, 2)
            dve.wait_ge(total_ready, 1)
            dve.scalar_tensor_tensor(out=var[:, :], in0=ps_tot[:, :], scalar=1.0 / NODES, in1=mean2[:, :],
                                     op0=ALU.mult, op1=ALU.subtract).then_inc(var_ready, 1)
            dve.wait_ge(rstd_ready, 1)
            dve.wait_ge(affine_loaded, 32)
            dve.tensor_tensor(scale[:, :], var[:, :], gam[:, :], ALU.mult).then_inc(chain, 1)
            dve.wait_ge(chain, 3)
            dve.tensor_tensor(mean2[:, :], mean[:, :], scale[:, :], ALU.mult).then_inc(chain, 1)
            dve.wait_ge(chain, 4)
            dve.tensor_tensor(shift[:, :], bet[:, :], mean2[:, :], ALU.subtract).then_inc(shift_ready, 1)
            dve.wait_ge(shift_ready, 1)

            for i, b in enumerate(order):
                n = BLOCKS[b][1]
                m = m_buf[:, buf_of(i), 0:n, :]
                dve.wait_ge(m_loaded[buf_of(i)], 16 * loads_of(i))
                dve.tensor_tensor(m, m, scale[:, :].unsqueeze(1).to_broadcast([P, n, F]), ALU.mult).then_inc(scaled, 1)
                dve.wait_ge(scaled, i + 1)
                if b < SPILLED_BLOCKS:
                    dve.wait_ge(y_loaded[b], 16)
                dve.tensor_tensor(m, m, y_of(b), ALU.add).then_inc(y_added, 1)
                dve.wait_ge(y_added, i + 1)
                dve.tensor_tensor(m, m, shift[:, :].unsqueeze(1).to_broadcast([P, n, F]), ALU.add).then_inc(shifted, 1)
                if i == 0:
                    dve.tensor_tensor(m_rest[:, :], m_rest[:, :], scale[0:N_REST, :], ALU.mult).then_inc(rest_done, 1)
                    dve.wait_ge(rest_done, 1)
                    dve.tensor_tensor(m_rest[:, :], m_rest[:, :], y_kept[0:N_REST, rest_row, :], ALU.add).then_inc(rest_done, 1)
                    dve.wait_ge(rest_done, 2)
                    dve.tensor_tensor(m_rest[:, :], m_rest[:, :], shift[0:N_REST, :], ALU.add).then_inc(rest_done, 1)


_INS = ["x", "src", "dst", "edge_attr_32", "L0_gnn_W_f", "L0_gnn_b_f", "L0_gnn_W_s", "L0_gnn_b_s",
        "L0_gnn_gamma", "L0_gnn_beta"]


def kernel(**inputs):
    import numpy as _np
    import concourse.bacc as _bacc
    from concourse.bass_utils import run_bass_kernel_spmd as _run

    nc = _bacc.Bacc("TRN2", target_bir_lowering=False, num_devices=1)
    arrays, args = {}, []
    for name in _INS:
        a = _np.ascontiguousarray(inputs[name])
        arrays[f"in_{name}_dram"] = a
        args.append(nc.dram_tensor(f"in_{name}_dram", a.shape, mybir.dt.from_np(a.dtype), kind="ExternalInput").ap())
    out = nc.dram_tensor("out_dram", (NODES, F), F32, kind="ExternalOutput").ap()
    msgs = nc.dram_tensor("msgs_dram", (NODES + DUMP, F), F32, kind="Internal").ap()
    y_spill = nc.dram_tensor("y_spill_dram", (P, SPILL * BULK, F), F32, kind="Internal").ap()
    build(nc, *args, out, msgs, y_spill)
    r = _run(nc, [arrays], core_ids=[0])
    return r.results[0]["out_dram"]
```

```python
from contextlib import ExitStack

import concourse.bass as bass
from concourse import mybir

F32 = mybir.dt.float32
BF16 = mybir.dt.bfloat16
I32 = mybir.dt.int32
ALU = mybir.AluOpType
ACT = mybir.ActivationFunctionType
AX = mybir.AxisListType

P = 128
NODES, EDGES, F, EF = 100000, 25000, 64, 32
EPS = 1e-5
TILES = 4
PAIRS = TILES // 2
GATHERED = 2 * TILES
BULK = 16
ROWS = GATHERED + BULK
E_COLS = EDGES // P
E_REST = EDGES - P * E_COLS
ALL_TILES = E_COLS + 1
GROUPS = ALL_TILES // TILES
LAST = GROUPS - 1
N_ROWS = NODES // P
N_REST = NODES - P * N_ROWS
LAST_ROWS = N_ROWS - BULK * LAST
UNROLL = 6
ITERS = LAST // UNROLL
SKEW = UNROLL - 1
STEPS = GROUPS + SKEW
SLOTS = 3
SPILL = 18
KEPT_ROWS = (GROUPS - SPILL) * BULK
ACC_LAG = 5
ZERO_PARTS = 12
ZERO_AHEAD = 3
DUMP = 3 * P
assert ALL_TILES == TILES * GROUPS and ITERS * UNROLL == LAST and UNROLL % SLOTS == 0
assert 0 < LAST_ROWS < BULK

S_BLK = 32
K_BLK = 32
BLOCKS = [(r, min(S_BLK, SPILL * BULK - r)) for r in range(0, SPILL * BULK, S_BLK)]
SPILLED_BLOCKS = len(BLOCKS)
BLOCKS += [(r, min(K_BLK, N_ROWS - r)) for r in range(SPILL * BULK, N_ROWS, K_BLK)]
NB = len(BLOCKS)
M_BUFS = 9
SQ_ROWS = 16
SQ_BUFS = 3
Y_ROWS = 32
BANK_ROWS = 8
SPLIT = 3


class Group:

    def __init__(self, it, off):
        self.it, self.off = it, off

    def back(self, n):
        return Group(self.it, self.off - n)

    @property
    def known(self):
        return isinstance(self.it, int)

    @property
    def n(self):
        return self.it * UNROLL + self.off

    def slot(self, ring):
        return self.off % ring

    def uses(self, ring):
        return self.it * (UNROLL // ring) + self.off // ring

    def exists(self):
        return not self.known or 0 <= self.n < GROUPS

    def nodes(self):
        return not self.known or SKEW <= self.n < STEPS

    @property
    def first_row(self):
        return 0 if self.exists() else GATHERED

    @property
    def end_row(self):
        return ROWS if self.nodes() else GATHERED


def wait_group(eng, sem, g, per=1):
    if not g.known or g.n >= 0:
        eng.wait_ge(sem, per * (g.n + 1) if per > 1 else g.n + 1)


def in_steps(g):
    return not g.known or 0 <= g.n < STEPS


def run_groups(eng, step, extra):
    for u in range(UNROLL):
        step(Group(0, u))
    with eng.Fori(1, ITERS) as it:
        for u in range(UNROLL):
            step(Group(it, u))
    for u in range(GROUPS - LAST + extra):
        step(Group(ITERS, u))


def build(nc, x, src, dst, ea, w_f, b_f, w_s, b_s, gamma, beta, out, msgs, y_spill):
    x_rows = x[0:P * N_ROWS, :].rearrange("(p r) f -> p r f", p=P)
    ea_tiles = ea[0:P * E_COLS, :].rearrange("(p t) f -> p t f", p=P)
    m_rows = msgs[0:P * N_ROWS, :].rearrange("(p r) f -> p r f", p=P)
    out_rows = out[0:P * N_ROWS, :].rearrange("(p r) f -> p r f", p=P)

    with ExitStack() as outer:
        def sem(name):
            return outer.enter_context(nc.semaphore(name))

        def keep(name, shape, dt=F32):
            return outer.enter_context(nc.sbuf_tensor(name, shape, dt))

        y_kept = keep("y_kept", [P, KEPT_ROWS, F])
        ones = keep("ones", [P, P])
        ident = keep("ident", [P, P])
        eps_col = keep("eps_col", [P, 1])
        one_col = keep("one_col", [P, 1])
        msg_sum = keep("msg_sum", [P, F])

        stage_one(nc, sem, x, src, dst, ea, w_f, b_f, w_s, b_s, msgs, y_spill,
                  x_rows, ea_tiles, m_rows, y_kept, ones, ident, eps_col, one_col, msg_sum)
        stage_two(nc, sem, msgs, y_spill, gamma, beta, out, m_rows, out_rows,
                  y_kept, ones, ident, eps_col, msg_sum)


def stage_one(nc, sem, x, src, dst, ea, w_f, b_f, w_s, b_s, msgs, y_spill,
              x_rows, ea_tiles, m_rows, y_kept, ones, ident, eps_col, one_col, msg_sum):
    with ExitStack() as ctx:
        def sb(name, shape, dt=F32):
            return ctx.enter_context(nc.sbuf_tensor(name, shape, dt))

        def ps(name, shape):
            return ctx.enter_context(nc.psum_tensor(name, shape, F32))

        ids = sb("ids", [P, 2, ALL_TILES], I32)
        src_f = sb("src_f", [P, ALL_TILES])
        dump_row = sb("dump_row", [P, TILES])
        small = sb("small", [P, 4])
        real = sb("real", [P, P])
        earlier = sb("earlier", [P, P])
        zeros = sb("zeros", [P, BULK * F])
        w_z = sb("w_z", [P, 2 * F])
        w_e = sb("w_e", [P, TILES, 2 * F])
        b_row = sb("b_row", [1, TILES, 2 * F])
        own = sb("own", [P, UNROLL, TILES])
        gidx = sb("gidx", [P, UNROLL, 2, TILES], I32)
        xg = sb("xg", [P, SLOTS, ROWS, F])
        eas = sb("eas", [P, SLOTS, TILES, EF])
        xc = sb("xc", [P, 2, ROWS, F])
        sq = sb("sq", [P, ROWS, F])
        row_sum = sb("row_sum", [P, ROWS])
        row_ssq = sb("row_ssq", [P, ROWS])
        row_lnv = sb("row_lnv", [P, ROWS])
        row_rstd = sb("row_rstd", [P, ROWS])
        z_t = sb("z_t", [P, TILES, P])
        ea_t = sb("ea_t", [P, P])
        spl = sb("spl", [P, TILES, 2 * F])
        soft = sb("soft", [P, TILES, 2 * F])
        gate = sb("gate", [P, TILES, F])
        msg = sb("msg", [P, TILES, F])
        same = sb("same", [P, PAIRS, 2, 2 * P])
        before = sb("before", [P, PAIRS, 2, P])
        gap = sb("gap", [P, TILES])
        moved = sb("moved", [P, TILES])
        target = sb("target", [P, UNROLL, TILES], I32)
        comb = sb("comb", [P, UNROLL, TILES, F])

        ps_z = ps("ps_z", [P, TILES, P])
        ps_e = ps("ps_e", [P, P])
        ps_v = [ps(f"ps_v{i}", [P, TILES, 2 * F]) for i in range(2)]
        ps_src = ps("ps_src", [P, TILES, P])
        ps_c = ps("ps_c", [P, TILES, F])
        ps_n = ps("ps_n", [P, TILES])
        ps_sum = ps("ps_sum", [P, F])

        ids_loaded = sem("ids_loaded")
        w_loaded = sem("w_loaded")
        w_cleared = sem("w_cleared")
        masks_set = sem("masks_set")
        masks_made = sem("masks_made")
        consts = sem("consts")
        prep = sem("prep")
        zeros_set = sem("zeros_set")
        table_zeroed = sem("table_zeroed")
        x_loaded = [sem(f"x_loaded{i}") for i in range(SLOTS)]
        ea_loaded = [sem(f"ea_loaded{i}") for i in range(SLOTS)]
        gathered = [sem(f"gathered{i}") for i in range(SLOTS)]
        staged = sem("staged")
        gathers_begun = sem("gathers_begun")
        own_staged = sem("own_staged")
        summed = sem("summed")
        centred = sem("centred")
        squared = sem("squared")
        ssq_done = sem("ssq_done")
        lnv_done = sem("lnv_done")
        rstd_done = sem("rstd_done")
        h_done = sem("h_done")
        y_done = sem("y_done")
        spilled = sem("spilled")
        ea_turned = sem("ea_turned")
        ea_copied = sem("ea_copied")
        z_turned = sem("z_turned")
        z_copied = sem("z_copied")
        v_done = sem("v_done")
        spl_steps = sem("spl_steps")
        spl_done = sem("spl_done")
        soft_done = sem("soft_done")
        gate_done = sem("gate_done")
        msg_done = sem("msg_done")
        src_spread = sem("src_spread")
        same_done = sem("same_done")
        before_done = sem("before_done")
        comb_done = sem("comb_done")
        comb_copied = sem("comb_copied")
        gap_done = sem("gap_done")
        moved_done = sem("moved_done")
        target_done = sem("target_done")
        accumulated = sem("accumulated")
        slots_free = sem("slots_free")
        sum_started = sem("sum_started")
        sum_kept = sem("sum_kept")

        X_LAST, EA_LAST = 2, 3

        block = ctx.enter_context(nc.Block())

        @block.sync
        def _(sp):
            for c, v in enumerate((src, dst)):
                sp.dma_start(ids[:, c, 0:E_COLS],
                             v[0:P * E_COLS].rearrange("(p t) -> p t", p=P)).then_inc(ids_loaded, 16)
                sp.dma_start(ids[0:E_REST, c, E_COLS:ALL_TILES],
                             v[P * E_COLS:EDGES].rearrange("(p t) -> p t", t=1)).then_inc(ids_loaded, 16)
                sp.dma_start(ids[E_REST:P, c, E_COLS:ALL_TILES],
                             v[0:P - E_REST].rearrange("(p t) -> p t", t=1)).then_inc(ids_loaded, 16)

            def load_nodes(g):
                slot = g.slot(SLOTS)
                wait_group(sp, y_done, g.back(SLOTS))
                if g.known and g.n == STEPS - 1:
                    sp.dma_start(xg[:, slot, GATHERED:GATHERED + LAST_ROWS, :],
                                 x_rows[:, BULK * LAST:N_ROWS, :]).then_inc(x_loaded[slot], 16)
                    sp.dma_start(xg[0:N_REST, slot, GATHERED + LAST_ROWS, :],
                                 x[P * N_ROWS:NODES, :]).then_inc(x_loaded[slot], 16)
                else:
                    sp.dma_start(xg[:, slot, GATHERED:ROWS, :],
                                 x_rows[:, bass.ds((g.n - SKEW) * BULK, BULK), :]).then_inc(x_loaded[slot], 16)

            def load_edges(g):
                slot = g.slot(SLOTS)
                wait_group(sp, ea_turned, g.back(SLOTS))
                if g.known and g.n == LAST:
                    sp.dma_start(eas[:, slot, 0:TILES - 1, :],
                                 ea_tiles[:, E_COLS - TILES + 1:E_COLS, :]).then_inc(ea_loaded[slot], 16)
                    sp.dma_start(eas[0:E_REST, slot, TILES - 1, :],
                                 ea[P * E_COLS:EDGES, :]).then_inc(ea_loaded[slot], 16)
                    sp.dma_start(eas[E_REST:P, slot, TILES - 1, :],
                                 ea[0:P - E_REST, :]).then_inc(ea_loaded[slot], 16)
                else:
                    sp.dma_start(eas[:, slot, :, :],
                                 ea_tiles[:, bass.ds(g.n * TILES, TILES), :]).then_inc(ea_loaded[slot], 16)

            def load(g):
                if g.nodes():
                    load_nodes(g)
                if g.exists():
                    load_edges(g)

            run_groups(sp, load, SKEW)

        @block.gpsimd
        def _(pool):
            pool.sem_inc(slots_free, PAIRS * UNROLL - 1)
            pool.memset(ident[:, :], 0.0).then_inc(masks_set, 1)
            pool.memset(earlier[:, :], 1.0).then_inc(masks_set, 1)
            pool.wait_ge(masks_set, 2)
            pool.affine_select(out=ident[:, :], in_=ident[:, :], compare_op=ALU.not_equal, fill=1.0,
                               base=0, pattern=[[-1, P]], channel_multiplier=1).then_inc(masks_made, 1)
            pool.affine_select(out=earlier[:, :], in_=earlier[:, :], compare_op=ALU.is_gt, fill=0.0,
                               base=0, pattern=[[1, P]], channel_multiplier=-1).then_inc(masks_made, 1)

            def gather(g, q):
                s = g.slot(SLOTS)
                for j in (2 * q, 2 * q + 1):
                    for c in range(2):
                        pool.indirect_dma_start(
                            xg[:, s, 2 * j + c, :], None, x,
                            bass.IndirectOffsetOnAxis(ap=gidx[:, g.slot(UNROLL), c, j:j + 1], axis=0),
                        ).then_inc(gathered[s], 16)

            def accumulate(g, q):
                if g.known:
                    pairs = g.n * PAIRS + q
                    if pairs:
                        pool.wait_ge(accumulated, 32 * pairs)
                else:
                    pool.wait_ge(accumulated, 32 * PAIRS * g.n + 32 * q)
                pool.sem_inc(slots_free, 1)
                for j in (2 * q, 2 * q + 1):
                    pool.indirect_dma_start(
                        msgs, bass.IndirectOffsetOnAxis(ap=target[:, g.slot(UNROLL), j:j + 1], axis=0),
                        comb[:, g.slot(UNROLL), j, :], None, compute_op=ALU.add,
                    ).then_inc(accumulated, 16)

            def step(g):
                old = g.back(ACC_LAG)
                if g.known and g.n == ACC_LAG:
                    pool.wait_ge(table_zeroed, 16 * (ZERO_PARTS + 2))
                if not g.known or g.n < GROUPS:
                    wait_group(pool, staged, g)
                    wait_group(pool, centred, g.back(SLOTS))
                    pool.sem_inc(gathers_begun, 1)
                    gather(g, 0)
                if old.exists():
                    wait_group(pool, comb_copied, old)
                    wait_group(pool, target_done, old)
                    accumulate(old, 0)
                if not g.known or g.n < GROUPS:
                    gather(g, 1)
                if old.exists():
                    accumulate(old, 1)

            for u in range(UNROLL):
                step(Group(0, u))
            with pool.Fori(1, ITERS) as it:
                for u in range(UNROLL):
                    step(Group(it, u))
            for u in range(1 + ACC_LAG):
                step(Group(ITERS, u))
            pool.wait_ge(accumulated, 16 * ALL_TILES)

        @block.vector
        def _(dve):
            dve.memset(zeros[:, :], 0.0).then_inc(zeros_set, 1)
            dve.memset(w_e[:, :, :], 0.0).then_inc(w_cleared, 1)
            dve.wait_ge(ids_loaded, 96)
            dve.tensor_copy(gidx[:, 0, :, :], ids[:, :, 0:TILES]).then_inc(staged, 1)
            dve.memset(ones[:, :], 1.0)
            dve.memset(one_col[:, :], 1.0)
            dve.memset(eps_col[:, :], EPS).then_inc(consts, 1)
            dve.wait_ge(masks_made, 2)
            dve.tensor_reduce(small[:, 0:1], earlier[:, :], AX.X, ALU.add).then_inc(prep, 1)
            dve.wait_ge(prep, 1)
            for j in range(TILES):
                dve.tensor_scalar(dump_row[:, j:j + 1], small[:, 0:1], float(NODES + P * (j % 2)), None, ALU.add)
            dve.tensor_scalar(small[:, 1:2], small[:, 0:1], float(P - 1 - E_REST) + 0.5, None, ALU.is_gt)
            dve.tensor_scalar(small[:, 2:3], small[:, 0:1], float(NODES + 2 * P), None, ALU.add)
            dve.tensor_copy(src_f[:, :], ids[:, 0, :]).then_inc(prep, 1)
            dve.wait_ge(prep, 2)
            dve.tensor_scalar(real[:, :], ones[:, :], small[:, 1:2], None, ALU.mult)
            dve.tensor_tensor(small[:, 3:4], src_f[:, E_COLS:ALL_TILES], small[:, 2:3],
                              ALU.subtract).then_inc(prep, 1)
            dve.wait_ge(prep, 3)
            dve.tensor_scalar(src_f[:, E_COLS:ALL_TILES], small[:, 3:4], small[:, 1:2], small[:, 2:3],
                              ALU.mult, ALU.add).then_inc(prep, 1)
            dve.wait_ge(prep, 4)
            dve.tensor_copy(own[:, 0, :], src_f[:, 0:TILES]).then_inc(own_staged, 1)
            def stage_indices(g):
                dve.tensor_copy(gidx[:, g.slot(UNROLL), :, :],
                                ids[:, :, bass.ds(g.n * TILES, TILES)]).then_inc(staged, 1)
                wait_group(dve, target_done, g.back(UNROLL))
                dve.tensor_copy(own[:, g.slot(UNROLL), :],
                                src_f[:, bass.ds(g.n * TILES, TILES)]).then_inc(own_staged, 1)

            def sums(g):
                slot, rows = g.slot(SLOTS), slice(g.first_row, g.end_row)
                if g.exists():
                    dve.wait_ge(gathered[slot], 16 * GATHERED * g.uses(SLOTS) + 16 * GATHERED)
                if g.nodes():
                    extra = 16 * (X_LAST - 1) if g.known and g.n == STEPS - 1 else 0
                    dve.wait_ge(x_loaded[slot], 16 * (g.uses(SLOTS) - len(range(slot, SKEW, SLOTS))) + 16 + extra)
                wait_group(dve, centred, g.back(1))
                dve.tensor_reduce(row_sum[:, rows], xg[:, slot, rows, :], AX.X, ALU.add).then_inc(summed, 1)

            def centre(g):
                wait_group(dve, summed, g)
                if g.back(2).exists():
                    wait_group(dve, z_turned, g.back(2))
                wait_group(dve, y_done, g.back(2))
                rows = slice(g.first_row, g.end_row)
                dve.scalar_tensor_tensor(
                    out=xc[:, g.slot(2), rows, :],
                    in0=row_sum[:, rows].unsqueeze(2).to_broadcast([P, g.end_row - g.first_row, F]),
                    scalar=-1.0 / F, in1=xg[:, g.slot(SLOTS), rows, :], op0=ALU.mult, op1=ALU.add,
                ).then_inc(centred, 1)

            def sum_squares(g):
                wait_group(dve, squared, g)
                wait_group(dve, lnv_done, g.back(1))
                rows = slice(g.first_row, g.end_row)
                dve.tensor_reduce(row_ssq[:, rows], sq[:, rows, :], AX.X, ALU.add).then_inc(ssq_done, 1)

            def same_source(g):
                wait_group(dve, src_spread, g)
                wait_group(dve, comb_done, g.back(1))
                cols = own[:, g.slot(UNROLL), :].rearrange("p (q b) -> p q b", q=PAIRS)
                for q in range(PAIRS):
                    ins = dve.tensor_tensor(
                        same[:, q, :, :],
                        ps_src[:, 2 * q:2 * q + 2, :].rearrange("p a i -> p (a i)").unsqueeze(1)
                        .to_broadcast([P, 2, 2 * P]),
                        cols[:, q, :].unsqueeze(2).to_broadcast([P, 2, 2 * P]), ALU.is_equal)
                ins.then_inc(same_done, 1)
                wait_group(dve, same_done, g)
                for a in range(2):
                    ins = dve.tensor_tensor(before[:, :, a, :], same[:, :, a, a * P:(a + 1) * P],
                                            earlier[:, :].unsqueeze(1).to_broadcast([P, PAIRS, P]), ALU.mult)
                ins.then_inc(before_done, 1)

            def targets(g):
                wait_group(dve, comb_done, g)
                rows = own[:, g.slot(UNROLL), :]
                wait_group(dve, moved_done, g.back(1))
                dve.tensor_tensor(gap[:, :], dump_row[:, :], rows, ALU.subtract).then_inc(gap_done, 1)
                wait_group(dve, gap_done, g)
                wait_group(dve, target_done, g.back(1))
                dve.scalar_tensor_tensor(out=moved[:, :], in0=ps_n[:, :], scalar=0.0, in1=gap[:, :],
                                         op0=ALU.is_gt, op1=ALU.mult).then_inc(moved_done, 1)
                wait_group(dve, moved_done, g)
                wait_group(dve, slots_free, g, PAIRS)
                dve.tensor_tensor(target[:, g.slot(UNROLL), :], moved[:, :], rows, ALU.add).then_inc(target_done, 1)

            def softplus(g):
                wait_group(dve, spl_done, g)
                wait_group(dve, msg_done, g.back(1))
                wait_group(dve, gate_done, g.back(1))
                dve.scalar_tensor_tensor(out=soft[:, :, :], in0=ps_v[g.slot(2)][:, :, :], scalar=0.0, in1=spl[:, :, :],
                                         op0=ALU.max, op1=ALU.add).then_inc(soft_done, 1)

            def normalise(g):
                wait_group(dve, rstd_done, g)
                rows = slice(g.first_row, g.end_row)
                h = xc[:, g.slot(2), rows, :]
                dve.scalar_tensor_tensor(out=h, in0=h, scalar=0.0,
                                         in1=row_rstd[:, rows].unsqueeze(2)
                                         .to_broadcast([P, g.end_row - g.first_row, F]),
                                         op0=ALU.max, op1=ALU.mult).then_inc(h_done, 1)

            def residual(g, spill):
                if not g.nodes():
                    dve.sem_inc(y_done, 1)
                    return
                wait_group(dve, h_done, g)
                if not spill:
                    dve.wait_ge(spilled, 16 * SPILL)
                row = (g.n - SKEW) * BULK - (0 if spill else SPILL * BULK)
                dve.tensor_tensor(y_kept[:, bass.ds(row, BULK), :], xc[:, g.slot(2), GATHERED:ROWS, :],
                                  xg[:, g.slot(SLOTS), GATHERED:ROWS, :], ALU.add).then_inc(y_done, 1)

            def message(g):
                wait_group(dve, gate_done, g)
                wait_group(dve, comb_done, g.back(1))
                dve.tensor_tensor(msg[:, :, :], gate[:, :, :], soft[:, :, F:2 * F], ALU.mult).then_inc(msg_done, 1)

            def step(g, spill):
                if g.back(3).exists():
                    message(g.back(3))
                if g.back(-1).exists():
                    stage_indices(g.back(-1))
                if in_steps(g.back(1)):
                    sum_squares(g.back(1))
                if in_steps(g):
                    sums(g)
                    centre(g)
                if in_steps(g.back(1)):
                    normalise(g.back(1))
                    residual(g.back(1), spill)
                if g.back(2).exists():
                    same_source(g.back(2))
                    softplus(g.back(2))
                if g.back(3).exists():
                    targets(g.back(3))

            step(Group(0, 0), True)
            dve.wait_ge(w_loaded, 16 * (4 + 2 * TILES + 2 * TILES))
            dve.tensor_scalar(w_z[:, 0:F], w_z[:, 0:F], -1.0, None, ALU.mult)
            dve.tensor_scalar(w_e[:, :, 0:F], w_e[:, :, 0:F], -1.0, None, ALU.mult)
            dve.tensor_scalar(b_row[:, :, 0:F], b_row[:, :, 0:F], -1.0, None, ALU.mult).then_inc(prep, 1)
            for u in range(1, UNROLL):
                step(Group(0, u), True)
            first_kept = (SPILL + 1 + SKEW) // UNROLL
            with dve.Fori(1, first_kept) as it:
                for u in range(UNROLL):
                    step(Group(it, u), True)
            with dve.Fori(first_kept, ITERS) as it:
                for u in range(UNROLL):
                    step(Group(it, u), False)
            for u in range(STEPS - LAST + 1):
                step(Group(ITERS, u), False)

        @block.scalar
        def _(act):
            act.preload_act_table_set("natural_log_exp_and_others")
            act.wait_ge(zeros_set, 1)
            whole = N_ROWS // BULK * BULK

            def zero_table(u):
                n = whole // ZERO_PARTS
                act.dma_start(m_rows[:, u * n:(u + 1) * n, :].rearrange("p (n r) f -> p n (r f)", r=BULK),
                              zeros[:, :].unsqueeze(1).to_broadcast([P, n // BULK, BULK * F])
                              ).then_inc(table_zeroed, 16)
                if u == ZERO_PARTS - 1:
                    act.dma_start(m_rows[:, whole:N_ROWS, :],
                                  zeros[:, 0:(N_ROWS - whole) * F].rearrange("p (r f) -> p r f", f=F)
                                  ).then_inc(table_zeroed, 16)
                    over = (N_REST + DUMP) // 32
                    act.dma_start(msgs[P * N_ROWS:NODES + DUMP, :].rearrange("(p r) f -> p (r f)", p=32),
                                  zeros[0:32, 0:over * F]).then_inc(table_zeroed, 16)

            act.wait_ge(consts, 1)

            def square(g):
                wait_group(act, centred, g)
                wait_group(act, ssq_done, g.back(1))
                rows = slice(g.first_row, g.end_row)
                act.activation(sq[:, rows, :], xc[:, g.slot(2), rows, :], ACT.Square).then_inc(squared, 1)

            def rstd(g):
                wait_group(act, ssq_done, g)
                wait_group(act, rstd_done, g.back(1))
                rows = slice(g.first_row, g.end_row)
                act.activation(row_lnv[:, rows], row_ssq[:, rows], ACT.Ln, bias=eps_col[:, 0:1],
                               scale=1.0 / F).then_inc(lnv_done, 1)
                wait_group(act, lnv_done, g)
                wait_group(act, h_done, g.back(1))
                act.activation(row_rstd[:, rows], row_lnv[:, rows], ACT.Exp, scale=-0.5).then_inc(rstd_done, 1)

            def gates(g):
                wait_group(act, soft_done, g)
                wait_group(act, msg_done, g.back(1))
                act.activation(gate[:, :, :], soft[:, :, 0:F], ACT.Exp, scale=-1.0).then_inc(gate_done, 1)

            def copy_turned(g):
                wait_group(act, ea_turned, g)
                wait_group(act, v_done, g.back(1))
                act.activation(ea_t[:, :], ps_e[:, :], ACT.Copy).then_inc(ea_copied, 1)
                wait_group(act, z_turned, g)
                act.activation(z_t[:, :, :], ps_z[:, :, :], ACT.Copy).then_inc(z_copied, 1)

            def softplus_log(g):
                wait_group(act, v_done, g)
                wait_group(act, soft_done, g.back(1))
                act.activation(spl[:, :, :], ps_v[g.slot(2)][:, :, :], ACT.Abs).then_inc(spl_steps, 1)
                act.wait_ge(spl_steps, 2 * g.n + 1)
                act.activation(spl[:, :, :], spl[:, :, :], ACT.Exp, scale=-1.0).then_inc(spl_steps, 1)
                act.wait_ge(spl_steps, 2 * g.n + 2)
                act.activation(spl[:, :, :], spl[:, :, :], ACT.Ln, bias=one_col[:, 0:1]).then_inc(spl_done, 1)

            def copy_comb(g):
                wait_group(act, comb_done, g)
                wait_group(act, slots_free, g, PAIRS)
                act.activation(comb[:, g.slot(UNROLL), :, :], ps_c[:, :, :], ACT.Copy).then_inc(comb_copied, 1)

            def spill(g):
                wait_group(act, y_done, g)
                row = (g.n - SKEW) * BULK
                act.dma_start(y_spill[:, bass.ds(row, BULK), :],
                              y_kept[:, bass.ds(row, BULK), :]).then_inc(spilled, 16)

            def step(g, spills):
                if in_steps(g.back(1)):
                    rstd(g.back(1))
                if g.back(2).exists():
                    softplus_log(g.back(2))
                if in_steps(g):
                    square(g)
                if g.back(1).exists():
                    copy_turned(g.back(1))
                if g.back(2).exists():
                    gates(g.back(2))
                if g.back(3).exists():
                    copy_comb(g.back(3))
                if spills and g.back(1).nodes():
                    spill(g.back(1))

            for u in range(ZERO_AHEAD):
                zero_table(u)
            act.wait_ge(w_cleared, 1)
            for c, (w, b) in enumerate(((w_f, b_f), (w_s, b_s))):
                cols = slice(c * F, (c + 1) * F)
                act.dma_start(w_z[0:F, cols], w[0:F, :]).then_inc(w_loaded, 16)
                act.dma_start(w_z[F:2 * F, cols], w[F:2 * F, :]).then_inc(w_loaded, 16)
                for j in range(TILES):
                    act.dma_start(w_e[j * EF:(j + 1) * EF, j, cols], w[2 * F:2 * F + EF, :]).then_inc(w_loaded, 16)
                    act.dma_start(b_row[0:1, j, cols], b.rearrange("(a f) -> a f", a=1)).then_inc(w_loaded, 16)
            for u in range(UNROLL):
                for k in range(ZERO_AHEAD + 2 * u, min(ZERO_AHEAD + 2 * u + 2, ZERO_PARTS)):
                    zero_table(k)
                step(Group(0, u), True)
            first_kept = (SPILL + 1 + SKEW) // UNROLL
            with act.Fori(1, first_kept) as it:
                for u in range(UNROLL):
                    step(Group(it, u), True)
            with act.Fori(first_kept, ITERS) as it:
                for u in range(UNROLL):
                    step(Group(it, u), False)
            for u in range(STEPS - LAST + 1):
                step(Group(ITERS, u), False)
            act.activation(msg_sum[:, :], ps_sum[:, :], ACT.Copy).then_inc(sum_kept, 1)
            act.wait_ge(spilled, 16 * SPILL)

        @block.tensor
        def _(pe):
            pe.wait_ge(masks_made, 2)
            pe.wait_ge(consts, 1)
            pe.wait_ge(prep, 5)
            pe.matmul(ps_sum[:, :], zeros[:, 0:P], zeros[:, 0:F], start=True, stop=True,
                      skip_group_check=True).then_inc(sum_started, 1)

            def turn_edges(g):
                extra = 16 * (EA_LAST - 1) if g.known and g.n == LAST else 0
                pe.wait_ge(ea_loaded[g.slot(SLOTS)], 16 * g.uses(SLOTS) + 16 + extra)
                wait_group(pe, ea_copied, g.back(1))
                pe.transpose(ps_e[:, :], eas[:, g.slot(SLOTS), :, :].rearrange("p t f -> p (t f)"),
                             ident[:, :]).then_inc(ea_turned, 1)

            def spread_sources(g):
                wait_group(pe, same_done, g.back(1))
                wait_group(pe, own_staged, g)
                for j in range(TILES):
                    ins = pe.matmul(ps_src[:, j, :], own[:, g.slot(UNROLL), j:j + 1].to_broadcast([P, P]),
                                    ident[:, :], start=True, stop=True)
                ins.then_inc(src_spread, 1)

            def turn_z(g):
                wait_group(pe, h_done, g)
                wait_group(pe, z_copied, g.back(1))
                for j in range(TILES):
                    ins = pe.transpose(ps_z[:, j, :],
                                       xc[:, g.slot(2), 2 * j:2 * j + 2, :].rearrange("p c f -> p (c f)"),
                                       ident[:, :])
                ins.then_inc(z_turned, 1)

            def products(g):
                wait_group(pe, soft_done, g.back(2))
                v = ps_v[g.slot(2)]
                wait_group(pe, ea_copied, g)
                wait_group(pe, z_copied, g)
                pe.matmul(v[:, :, :].rearrange("p t f -> p (t f)"), ones[0:1, :],
                          b_row[0:1, :, :].rearrange("p t f -> p (t f)"), start=True, stop=True)
                for j in range(TILES):
                    pe.matmul(v[:, j, :], ea_t[:, :], w_e[:, j, :], start=False, stop=True,
                              skip_group_check=True)
                    ins = pe.matmul(v[:, j, :], z_t[:, j, :], w_z[:, :], start=False, stop=True,
                                    skip_group_check=True)
                ins.then_inc(v_done, 1)

            def combine(g):
                wait_group(pe, before_done, g)
                wait_group(pe, msg_done, g)
                wait_group(pe, comb_copied, g.back(1))
                wait_group(pe, moved_done, g.back(1))
                for q in range(PAIRS):
                    for a in range(2):
                        j = 2 * q + a
                        for b in range(2):
                            pe.matmul(ps_c[:, j, :], same[:, q, b, a * P:(a + 1) * P], msg[:, 2 * q + b, :],
                                      start=(b == 0), stop=(b == 1))
                        if a == 1:
                            pe.matmul(ps_n[:, j:j + 1], same[:, q, 0, P:2 * P], ones[:, 0:1],
                                      start=True, stop=False)
                        pe.matmul(ps_n[:, j:j + 1], before[:, q, a, :], ones[:, 0:1],
                                  start=(a == 0), stop=True)
                last = g.known and g.n == LAST
                for j in range(TILES):
                    w = real if last and j == TILES - 1 else ones
                    ins = pe.matmul(ps_sum[:, :], w[:, :], msg[:, j, :], start=False, stop=True, skip_group_check=True)
                ins.then_inc(comb_done, 1)

            def step(g):
                if g.back(3).exists():
                    combine(g.back(3))
                if g.back(1).exists():
                    turn_edges(g.back(1))
                    turn_z(g.back(1))
                    products(g.back(1))
                    spread_sources(g.back(1))

            run_groups(pe, step, 3)


def stage_two(nc, sem, msgs, y_spill, gamma, beta, out, m_rows, out_rows, y_kept, ones, ident, eps_col, msg_sum):
    with ExitStack() as ctx:
        def sb(name, shape, dt=F32):
            return ctx.enter_context(nc.sbuf_tensor(name, shape, dt))

        m_buf = sb("m_buf", [P, M_BUFS, max(n for _, n in BLOCKS), F])
        m_rest = sb("m_rest", [N_REST, F])
        sq_acc = sb("sq_acc", [P, SQ_ROWS, F])
        sq_row = sb("sq_row", [P, F])
        gam = sb("gam", [P, F])
        bet = sb("bet", [P, F])
        mean = sb("mean", [P, F])
        mean2 = sb("mean2", [P, F])
        var = sb("var", [P, F])
        lnv = sb("lnv", [P, F])
        scale = sb("scale", [P, F])
        shift = sb("shift", [P, F])
        part = sb("part", [P, SPLIT, F], BF16)
        left = sb("left", [P, SPLIT, F])
        shift_rows = sb("shift_rows", [P, BANK_ROWS, F], BF16)
        ones_b = sb("ones_b", [SPLIT, P], BF16)
        ps_all = ctx.enter_context(nc.psum_tensor("ps_all", [P, 2 * Y_ROWS, F], F32))
        ps_sq = [ps_all[:, i * SQ_ROWS:(i + 1) * SQ_ROWS, :] for i in range(SQ_BUFS)]
        ps_tot = ps_all[:, SQ_BUFS * SQ_ROWS, :]
        ps_y = [ps_all[:, i * Y_ROWS:(i + 1) * Y_ROWS, :] for i in range(2)]

        m_loaded = [sem(f"m_loaded{i}") for i in range(M_BUFS)]
        rest_loaded = sem("rest_loaded")
        affine_loaded = sem("affine_loaded")
        y_loaded = [sem(f"y_loaded{i}") for i in range(SPILLED_BLOCKS)]
        block_squared = sem("block_squared")
        part_squared = sem("part_squared")
        part_cleared = sem("part_cleared")
        part_added = sem("part_added")
        acc_reduced = sem("acc_reduced")
        total_ready = sem("total_ready")
        var_ready = sem("var_ready")
        ln_ready = sem("ln_ready")
        rstd_ready = sem("rstd_ready")
        chain = sem("chain")
        shift_ready = sem("shift_ready")
        split_done = sem("split_done")
        scaled = sem("scaled")
        y_summed = sem("y_summed")
        added = sem("added")
        rest_done = sem("rest_done")
        stored = [sem(f"stored{i}") for i in range(M_BUFS)]
        rest_stored = sem("rest_stored")

        parts = [(b, r, min(SQ_ROWS, n - r)) for b, (_, n) in enumerate(BLOCKS) for r in range(0, n, SQ_ROWS)]
        held = list(range(NB - M_BUFS, NB))
        order = held + list(range(SPILLED_BLOCKS, NB - M_BUFS)) + list(range(SPILLED_BLOCKS))
        assert len(order) == NB
        rest_row = (LAST - SPILL) * BULK + LAST_ROWS

        def buf_of(i):
            return order[i] % M_BUFS if i < M_BUFS else order[i % M_BUFS] % M_BUFS

        def loads_of(i):
            b = buf_of(i)
            return len([k for k in range(NB) if k % M_BUFS == b]) + len(
                [k for k in range(M_BUFS, i + 1) if buf_of(k) == b])

        def stores_of(i):
            return len([k for k in range(i + 1) if buf_of(k) == buf_of(i)])

        def y_of(b):
            r0, n = BLOCKS[b]
            if b >= SPILLED_BLOCKS:
                return y_kept[:, r0 - SPILL * BULK:r0 - SPILL * BULK + n, :]
            return y_kept[:, b * S_BLK:b * S_BLK + n, :]

        takes = {}
        for b in range(SPILLED_BLOCKS):
            lo, hi = b * S_BLK, b * S_BLK + BLOCKS[b][1]
            over = [i for i, k in enumerate(order) if k >= SPILLED_BLOCKS
                    and BLOCKS[k][0] - SPILL * BULK < hi and BLOCKS[k][0] - SPILL * BULK + BLOCKS[k][1] > lo]
            takes[b] = max(over)

        y_parts = [(i, r, min(Y_ROWS, BLOCKS[b][1] - r)) for i, b in enumerate(order)
                   for r in range(0, BLOCKS[b][1], Y_ROWS)]

        def sums_of(i):
            return len([k for k, _, _ in y_parts if k <= i])

        block = ctx.enter_context(nc.Block())

        @block.sync
        def _(sp):
            for b, (r0, n) in enumerate(BLOCKS):
                if b >= M_BUFS:
                    sp.wait_ge(block_squared, b - M_BUFS + 1)
                sp.dma_start(m_buf[:, b % M_BUFS, 0:n, :], m_rows[:, r0:r0 + n, :]).then_inc(m_loaded[b % M_BUFS], 16)
            sp.dma_start(m_rest[:, :], msgs[P * N_ROWS:NODES, :]).then_inc(rest_loaded, 16)
            sp.dma_start(gam[:, :], gamma.rearrange("(a f) -> a f", a=1).to_broadcast([P, F])).then_inc(affine_loaded, 16)
            sp.dma_start(bet[:, :], beta.rearrange("(a f) -> a f", a=1).to_broadcast([P, F])).then_inc(affine_loaded, 16)
            for i in range(M_BUFS, NB):
                b = order[i]
                r0, n = BLOCKS[b]
                if b < SPILLED_BLOCKS:
                    sp.wait_ge(y_summed, sums_of(takes[b]))
                    sp.dma_start(y_of(b), y_spill[:, r0:r0 + n, :]).then_inc(y_loaded[b], 16)
                sp.wait_ge(stored[buf_of(i)], 16 * stores_of(i - M_BUFS))
                sp.dma_start(m_buf[:, buf_of(i), 0:n, :], m_rows[:, r0:r0 + n, :]).then_inc(m_loaded[buf_of(i)], 16)

        @block.scalar
        def _(act):
            for k, (b, r, n) in enumerate(parts):
                if r == 0:
                    act.wait_ge(m_loaded[b % M_BUFS], 16 * (b // M_BUFS + 1))
                if k >= SQ_BUFS:
                    act.wait_ge(part_added, k - SQ_BUFS + 1)
                ins = act.activation(ps_sq[k % SQ_BUFS][:, 0:n, :], m_buf[:, b % M_BUFS, r:r + n, :], ACT.Square)
                ins.then_inc(part_squared, 1)
                if r + n == BLOCKS[b][1]:
                    act.wait_ge(part_squared, k + 1)
                    act.sem_inc(block_squared, 1)
            act.wait_ge(rest_loaded, 16)
            act.wait_ge(part_added, len(parts) - SQ_BUFS + 1)
            act.activation(ps_sq[len(parts) % SQ_BUFS][0:N_REST, 0, :], m_rest[:, :], ACT.Square).then_inc(part_squared, 1)
            act.wait_ge(var_ready, 1)
            act.activation(lnv[:, :], var[:, :], ACT.Ln, bias=eps_col[:, 0:1]).then_inc(ln_ready, 1)
            act.wait_ge(ln_ready, 1)
            act.activation(var[:, :], lnv[:, :], ACT.Exp, scale=-0.5).then_inc(rstd_ready, 1)
            for i, b in enumerate(order):
                r0, n = BLOCKS[b]
                act.wait_ge(added, sums_of(i))
                act.dma_start(out_rows[:, r0:r0 + n, :], m_buf[:, buf_of(i), 0:n, :]).then_inc(stored[buf_of(i)], 16)
            act.wait_ge(rest_done, 3)
            act.dma_start(out[P * N_ROWS:NODES, :], m_rest[:, :]).then_inc(rest_stored, 16)
            for k in range(M_BUFS):
                last = max(i for i in range(NB) if buf_of(i) == k)
                act.wait_ge(stored[k], 16 * stores_of(last))
            act.wait_ge(rest_stored, 16)

        @block.tensor
        def _(pe):
            pe.wait_ge(acc_reduced, 1)
            pe.matmul(ps_tot, ones[:, :], sq_row[:, :], start=True, stop=True).then_inc(total_ready, 1)
            pe.wait_ge(split_done, SPLIT + 1)
            for k, (i, r, n) in enumerate(y_parts):
                b = order[i]
                if b < SPILLED_BLOCKS:
                    pe.wait_ge(y_loaded[b], 16)
                if k >= 2:
                    pe.wait_ge(added, k - 1)
                for c in range(0, n, BANK_ROWS):
                    w = min(BANK_ROWS, n - c)
                    to = ps_y[k % 2][:, c:c + w, :].rearrange("p r f -> p (r f)")
                    pe.matmul(to, ident[:, :], y_of(b)[:, r + c:r + c + w, :].rearrange("p r f -> p (r f)"),
                              start=True, stop=False)
                    ins = pe.matmul(to, ones_b[:, :], shift_rows[0:SPLIT, 0:w, :].rearrange("p r f -> p (r f)"),
                                    start=False, stop=True)
                ins.then_inc(y_summed, 1)

        @block.vector
        def _(dve):
            dve.memset(sq_acc[:, :, :], 0.0).then_inc(part_cleared, 1)
            dve.wait_ge(part_cleared, 1)
            for k, (b, r, n) in enumerate(parts):
                dve.wait_ge(part_squared, k + 1)
                if k:
                    dve.wait_ge(part_added, k)
                dve.tensor_tensor(sq_acc[:, 0:n, :], sq_acc[:, 0:n, :], ps_sq[k % SQ_BUFS][:, 0:n, :],
                                  ALU.add).then_inc(part_added, 1)
            k = len(parts)
            dve.wait_ge(part_squared, k + 1)
            dve.wait_ge(part_added, k)
            dve.tensor_tensor(sq_acc[0:N_REST, 0, :], sq_acc[0:N_REST, 0, :], ps_sq[k % SQ_BUFS][0:N_REST, 0, :],
                              ALU.add).then_inc(part_added, 1)
            dve.wait_ge(part_added, k + 1)
            dve.tensor_reduce(sq_row[:, :], sq_acc[:, :, :].rearrange("p r f -> p f r"), AX.X,
                              ALU.add).then_inc(acc_reduced, 1)
            dve.tensor_scalar(mean[:, :], msg_sum[:, :], 1.0 / NODES, None, ALU.mult).then_inc(chain, 1)
            dve.wait_ge(chain, 1)
            dve.tensor_tensor(mean2[:, :], mean[:, :], mean[:, :], ALU.mult).then_inc(chain, 1)
            dve.wait_ge(chain, 2)
            dve.wait_ge(total_ready, 1)
            dve.scalar_tensor_tensor(out=var[:, :], in0=ps_tot, scalar=1.0 / NODES, in1=mean2[:, :],
                                     op0=ALU.mult, op1=ALU.subtract).then_inc(var_ready, 1)
            dve.wait_ge(rstd_ready, 1)
            dve.wait_ge(affine_loaded, 32)
            dve.tensor_tensor(scale[:, :], var[:, :], gam[:, :], ALU.mult).then_inc(chain, 1)
            dve.wait_ge(chain, 3)
            dve.tensor_tensor(mean2[:, :], mean[:, :], scale[:, :], ALU.mult).then_inc(chain, 1)
            dve.wait_ge(chain, 4)
            dve.tensor_tensor(shift[:, :], bet[:, :], mean2[:, :], ALU.subtract).then_inc(shift_ready, 1)
            dve.wait_ge(shift_ready, 1)

            dve.memset(ones_b[:, :], 1.0)
            for k in range(SPLIT):
                dve.tensor_copy(part[:, k, :], shift[:, :] if k == 0 else left[:, k, :]).then_inc(chain, 1)
                dve.wait_ge(chain, 5 + 2 * k)
                if k < SPLIT - 1:
                    dve.tensor_tensor(left[:, k + 1, :], shift[:, :] if k == 0 else left[:, k, :], part[:, k, :],
                                      ALU.subtract).then_inc(chain, 1)
                    dve.wait_ge(chain, 6 + 2 * k)
            rows = shift_rows[:, :, :]
            for k in range(SPLIT):
                own_part = part[:, k, :].unsqueeze(1).to_broadcast([P, BANK_ROWS, F])
                if k == 0:
                    ins = dve.tensor_scalar(rows, own_part, ident[:, k:k + 1], None, ALU.mult)
                else:
                    ins = dve.scalar_tensor_tensor(out=rows, in0=own_part, scalar=ident[:, k:k + 1], in1=rows,
                                                   op0=ALU.mult, op1=ALU.add)
                ins.then_inc(split_done, 1)
                dve.wait_ge(split_done, k + 1)
            dve.sem_inc(split_done, 1)

            dve.tensor_tensor(m_rest[:, :], m_rest[:, :], scale[0:N_REST, :], ALU.mult).then_inc(rest_done, 1)
            dve.wait_ge(rest_done, 1)
            dve.tensor_tensor(m_rest[:, :], m_rest[:, :], y_kept[0:N_REST, rest_row, :], ALU.add).then_inc(rest_done, 1)
            dve.wait_ge(rest_done, 2)
            dve.tensor_tensor(m_rest[:, :], m_rest[:, :], shift[0:N_REST, :], ALU.add).then_inc(rest_done, 1)

            k = 0
            for i, b in enumerate(order):
                n = BLOCKS[b][1]
                m = m_buf[:, buf_of(i), 0:n, :]
                dve.wait_ge(m_loaded[buf_of(i)], 16 * loads_of(i))
                dve.tensor_tensor(m, m, scale[:, :].unsqueeze(1).to_broadcast([P, n, F]), ALU.mult).then_inc(scaled, 1)
                dve.wait_ge(scaled, i + 1)
                while k < len(y_parts) and y_parts[k][0] == i:
                    _, r, w = y_parts[k]
                    dve.wait_ge(y_summed, k + 1)
                    dve.tensor_tensor(m[:, r:r + w, :], m[:, r:r + w, :], ps_y[k % 2][:, 0:w, :],
                                      ALU.add).then_inc(added, 1)
                    k += 1


_INS = ["x", "src", "dst", "edge_attr_32", "L0_gnn_W_f", "L0_gnn_b_f", "L0_gnn_W_s", "L0_gnn_b_s",
        "L0_gnn_gamma", "L0_gnn_beta"]


def kernel(**inputs):
    import numpy as _np
    import concourse.bacc as _bacc
    from concourse.bass_utils import run_bass_kernel_spmd as _run

    nc = _bacc.Bacc("TRN2", target_bir_lowering=False, num_devices=1)
    arrays, args = {}, []
    for name in _INS:
        a = _np.ascontiguousarray(inputs[name])
        arrays[f"in_{name}_dram"] = a
        args.append(nc.dram_tensor(f"in_{name}_dram", a.shape, mybir.dt.from_np(a.dtype), kind="ExternalInput").ap())
    out = nc.dram_tensor("out_dram", (NODES, F), F32, kind="ExternalOutput").ap()
    msgs = nc.dram_tensor("msgs_dram", (NODES + DUMP, F), F32, kind="Internal").ap()
    y_spill = nc.dram_tensor("y_spill_dram", (P, SPILL * BULK, F), F32, kind="Internal").ap()
    build(nc, *args, out, msgs, y_spill)
    r = _run(nc, [arrays], core_ids=[0])
    return r.results[0]["out_dram"]
```

```python
from contextlib import ExitStack

import concourse.bass as bass
from concourse import mybir

F32 = mybir.dt.float32
BF16 = mybir.dt.bfloat16
I32 = mybir.dt.int32
ALU = mybir.AluOpType
ACT = mybir.ActivationFunctionType
AX = mybir.AxisListType

P = 128
NODES, EDGES, F, EF = 100000, 25000, 64, 32
EPS = 1e-5
TILES = 4
GATHERED = 2 * TILES
BULK = 16
ROWS = GATHERED + BULK
E_COLS = EDGES // P
E_REST = EDGES - P * E_COLS
ALL_TILES = E_COLS + 1
GROUPS = ALL_TILES // TILES
LAST = GROUPS - 1
N_ROWS = NODES // P
N_REST = NODES - P * N_ROWS
LAST_ROWS = N_ROWS - BULK * LAST
UNROLL = 6
ITERS = LAST // UNROLL
SKEW = 4
STEPS = GROUPS + SKEW
SLOTS = 3
SPILL = 19
KEPT_ROWS = (GROUPS - SPILL) * BULK
ACC_LAG = 7
ZERO_PARTS = 16
ZERO_AHEAD = 4
DUMP = (TILES + 1) * P
assert ALL_TILES == TILES * GROUPS and ITERS * UNROLL == LAST and UNROLL % SLOTS == 0
assert 0 < LAST_ROWS < BULK
assert (SPILL + 1 + SKEW) % UNROLL == 0

S_BLK = 32
K_BLK = 32
BLOCKS = [(r, min(S_BLK, SPILL * BULK - r)) for r in range(0, SPILL * BULK, S_BLK)]
SPILLED_BLOCKS = len(BLOCKS)
BLOCKS += [(r, min(K_BLK, N_ROWS - r)) for r in range(SPILL * BULK, N_ROWS, K_BLK)]
NB = len(BLOCKS)
M_BUFS = 9
SQ_ROWS = 16
SQ_BUFS = 3
Y_ROWS = 32
BANK_ROWS = 8
SPLIT = 3


class Group:

    def __init__(self, it, off):
        self.it, self.off = it, off

    def back(self, n):
        return Group(self.it, self.off - n)

    @property
    def known(self):
        return isinstance(self.it, int)

    @property
    def n(self):
        return self.it * UNROLL + self.off

    def slot(self, ring):
        return self.off % ring

    def uses(self, ring):
        return self.it * (UNROLL // ring) + self.off // ring

    def exists(self):
        return not self.known or 0 <= self.n < GROUPS

    def nodes(self):
        return not self.known or SKEW <= self.n < STEPS

    @property
    def first_row(self):
        return 0 if self.exists() else GATHERED

    @property
    def end_row(self):
        return ROWS if self.nodes() else GATHERED


def wait_group(eng, sem, g, per=1):
    if not g.known or g.n >= 0:
        eng.wait_ge(sem, per * (g.n + 1) if per > 1 else g.n + 1)


def in_steps(g):
    return not g.known or 0 <= g.n < STEPS


def run_groups(eng, step, extra):
    for u in range(UNROLL):
        step(Group(0, u))
    with eng.Fori(1, ITERS) as it:
        for u in range(UNROLL):
            step(Group(it, u))
    for u in range(GROUPS - LAST + extra):
        step(Group(ITERS, u))


def build(nc, x, src, dst, ea, w_f, b_f, w_s, b_s, gamma, beta, out, msgs, y_spill):
    x_rows = x[0:P * N_ROWS, :].rearrange("(p r) f -> p r f", p=P)
    ea_tiles = ea[0:P * E_COLS, :].rearrange("(p t) f -> p t f", p=P)
    m_rows = msgs[0:P * N_ROWS, :].rearrange("(p r) f -> p r f", p=P)
    out_rows = out[0:P * N_ROWS, :].rearrange("(p r) f -> p r f", p=P)

    with ExitStack() as outer:
        def sem(name):
            return outer.enter_context(nc.semaphore(name))

        def keep(name, shape, dt=F32):
            return outer.enter_context(nc.sbuf_tensor(name, shape, dt))

        y_kept = keep("y_kept", [P, KEPT_ROWS, F])
        ones = keep("ones", [P, P])
        ident = keep("ident", [P, P])
        eps_col = keep("eps_col", [P, 1])
        one_col = keep("one_col", [P, 1])
        msg_sum = keep("msg_sum", [P, F])

        stage_one(nc, sem, x, src, dst, ea, w_f, b_f, w_s, b_s, msgs, y_spill,
                  x_rows, ea_tiles, m_rows, y_kept, ones, ident, eps_col, one_col, msg_sum)
        stage_two(nc, sem, msgs, y_spill, gamma, beta, out, m_rows, out_rows,
                  y_kept, ones, ident, eps_col, msg_sum)


def stage_one(nc, sem, x, src, dst, ea, w_f, b_f, w_s, b_s, msgs, y_spill,
              x_rows, ea_tiles, m_rows, y_kept, ones, ident, eps_col, one_col, msg_sum):
    with ExitStack() as ctx:
        def sb(name, shape, dt=F32):
            return ctx.enter_context(nc.sbuf_tensor(name, shape, dt))

        def ps(name, shape):
            return ctx.enter_context(nc.psum_tensor(name, shape, F32))

        ids = sb("ids", [P, 2, ALL_TILES], I32)
        src_f = sb("src_f", [P, ALL_TILES])
        dump_row = sb("dump_row", [P, TILES])
        small = sb("small", [P, 4])
        real = sb("real", [P, P])
        upto = sb("upto", [P, P])
        zeros = sb("zeros", [P, BULK * F])
        w_z = sb("w_z", [P, 2 * F])
        w_e = sb("w_e", [P, TILES, 2 * F])
        b_row = sb("b_row", [1, TILES, 2 * F])
        own = sb("own", [P, UNROLL, TILES])
        gidx = sb("gidx", [P, UNROLL, 2, TILES], I32)
        xg = sb("xg", [P, SLOTS, ROWS, F])
        eas = sb("eas", [P, SLOTS, TILES, EF])
        xc = sb("xc", [P, 2, ROWS, F])
        sq = sb("sq", [P, ROWS, F])
        row_sum = sb("row_sum", [P, ROWS])
        row_ssq = sb("row_ssq", [P, ROWS])
        row_lnv = sb("row_lnv", [P, ROWS])
        row_rstd = sb("row_rstd", [P, ROWS])
        z_t = sb("z_t", [P, TILES, P])
        ea_t = sb("ea_t", [P, P])
        spl = sb("spl", [P, TILES, 2 * F])
        soft = sb("soft", [P, TILES, 2 * F])
        gate = sb("gate", [P, TILES, F])
        msg = sb("msg", [P, TILES, F])
        same = sb("same", [P, TILES, TILES, P])
        not_later = sb("not_later", [P, TILES, P])
        matches = sb("matches", [P, TILES])
        no_later = sb("no_later", [P, TILES])
        later = sb("later", [P, TILES])
        gap = sb("gap", [P, TILES])
        moved = sb("moved", [P, TILES])
        target = sb("target", [P, UNROLL, TILES], I32)
        comb = sb("comb", [P, UNROLL, TILES, F])

        ps_z = ps("ps_z", [P, TILES, P])
        ps_e = ps("ps_e", [P, P])
        ps_v = [ps(f"ps_v{i}", [P, TILES, 2 * F]) for i in range(2)]
        ps_src = ps("ps_src", [P, TILES, P])
        ps_c = ps("ps_c", [P, TILES, F])
        ps_sum = ps("ps_sum", [P, F])

        ids_loaded = sem("ids_loaded")
        w_loaded = sem("w_loaded")
        w_cleared = sem("w_cleared")
        masks_set = sem("masks_set")
        masks_made = sem("masks_made")
        consts = sem("consts")
        prep = sem("prep")
        zeros_set = sem("zeros_set")
        table_zeroed = sem("table_zeroed")
        x_loaded = [sem(f"x_loaded{i}") for i in range(SLOTS)]
        ea_loaded = [sem(f"ea_loaded{i}") for i in range(SLOTS)]
        gathered = [sem(f"gathered{i}") for i in range(SLOTS)]
        staged = sem("staged")
        gathers_begun = sem("gathers_begun")
        own_staged = sem("own_staged")
        summed = sem("summed")
        centred = sem("centred")
        squared = sem("squared")
        ssq_done = sem("ssq_done")
        lnv_done = sem("lnv_done")
        rstd_done = sem("rstd_done")
        h_done = sem("h_done")
        y_done = sem("y_done")
        spilled = sem("spilled")
        ea_turned = sem("ea_turned")
        ea_copied = sem("ea_copied")
        z_turned = sem("z_turned")
        z_copied = sem("z_copied")
        v_done = sem("v_done")
        spl_steps = sem("spl_steps")
        spl_done = sem("spl_done")
        soft_done = sem("soft_done")
        gate_done = sem("gate_done")
        msg_done = sem("msg_done")
        src_spread = sem("src_spread")
        same_done = sem("same_done")
        same_steps = sem("same_steps")
        not_later_done = sem("not_later_done")
        later_done = sem("later_done")
        comb_done = sem("comb_done")
        comb_copied = sem("comb_copied")
        gap_done = sem("gap_done")
        moved_done = sem("moved_done")
        target_done = sem("target_done")
        accumulated = sem("accumulated")
        slots_free = sem("slots_free")
        sum_started = sem("sum_started")
        sum_kept = sem("sum_kept")

        X_LAST, EA_LAST = 2, 3

        block = ctx.enter_context(nc.Block())

        @block.sync
        def _(sp):
            for c, v in enumerate((src, dst)):
                sp.dma_start(ids[:, c, 0:E_COLS],
                             v[0:P * E_COLS].rearrange("(p t) -> p t", p=P)).then_inc(ids_loaded, 16)
                sp.dma_start(ids[0:E_REST, c, E_COLS:ALL_TILES],
                             v[P * E_COLS:EDGES].rearrange("(p t) -> p t", t=1)).then_inc(ids_loaded, 16)
                sp.dma_start(ids[E_REST:P, c, E_COLS:ALL_TILES],
                             v[0:P - E_REST].rearrange("(p t) -> p t", t=1)).then_inc(ids_loaded, 16)

            def load_nodes(g):
                slot = g.slot(SLOTS)
                wait_group(sp, y_done, g.back(SLOTS))
                if g.known and g.n == STEPS - 1:
                    sp.dma_start(xg[:, slot, GATHERED:GATHERED + LAST_ROWS, :],
                                 x_rows[:, BULK * LAST:N_ROWS, :]).then_inc(x_loaded[slot], 16)
                    sp.dma_start(xg[0:N_REST, slot, GATHERED + LAST_ROWS, :],
                                 x[P * N_ROWS:NODES, :]).then_inc(x_loaded[slot], 16)
                else:
                    sp.dma_start(xg[:, slot, GATHERED:ROWS, :],
                                 x_rows[:, bass.ds((g.n - SKEW) * BULK, BULK), :]).then_inc(x_loaded[slot], 16)

            def load_edges(g):
                slot = g.slot(SLOTS)
                wait_group(sp, ea_turned, g.back(SLOTS))
                if g.known and g.n == LAST:
                    sp.dma_start(eas[:, slot, 0:TILES - 1, :],
                                 ea_tiles[:, E_COLS - TILES + 1:E_COLS, :]).then_inc(ea_loaded[slot], 16)
                    sp.dma_start(eas[0:E_REST, slot, TILES - 1, :],
                                 ea[P * E_COLS:EDGES, :]).then_inc(ea_loaded[slot], 16)
                    sp.dma_start(eas[E_REST:P, slot, TILES - 1, :],
                                 ea[0:P - E_REST, :]).then_inc(ea_loaded[slot], 16)
                else:
                    sp.dma_start(eas[:, slot, :, :],
                                 ea_tiles[:, bass.ds(g.n * TILES, TILES), :]).then_inc(ea_loaded[slot], 16)

            def load(g):
                if g.nodes():
                    load_nodes(g)
                if g.exists():
                    load_edges(g)

            run_groups(sp, load, SKEW)

        @block.gpsimd
        def _(pool):
            pool.sem_inc(slots_free, UNROLL - 1)
            pool.memset(ident[:, :], 0.0).then_inc(masks_set, 1)
            pool.memset(upto[:, :], 1.0).then_inc(masks_set, 1)
            pool.wait_ge(masks_set, 2)
            pool.affine_select(out=ident[:, :], in_=ident[:, :], compare_op=ALU.not_equal, fill=1.0,
                               base=0, pattern=[[-1, P]], channel_multiplier=1).then_inc(masks_made, 1)
            pool.affine_select(out=upto[:, :], in_=upto[:, :], compare_op=ALU.is_ge, fill=0.0,
                               base=0, pattern=[[-1, P]], channel_multiplier=1).then_inc(masks_made, 1)

            def gather(g):
                slot = g.slot(SLOTS)
                for j in range(TILES):
                    for c in range(2):
                        pool.indirect_dma_start(
                            xg[:, slot, 2 * j + c, :], None, x,
                            bass.IndirectOffsetOnAxis(ap=gidx[:, g.slot(UNROLL), c, j:j + 1], axis=0),
                        ).then_inc(gathered[slot], 16)

            def accumulate(g):
                wait_group(pool, comb_copied, g)
                wait_group(pool, target_done, g)
                wait_group(pool, accumulated, g.back(1), 16 * TILES)
                pool.sem_inc(slots_free, 1)
                for j in range(TILES):
                    pool.indirect_dma_start(
                        msgs, bass.IndirectOffsetOnAxis(ap=target[:, g.slot(UNROLL), j:j + 1], axis=0),
                        comb[:, g.slot(UNROLL), j, :], None, compute_op=ALU.add,
                    ).then_inc(accumulated, 16)

            def step(g):
                if not g.known or g.n < GROUPS:
                    wait_group(pool, staged, g)
                    wait_group(pool, centred, g.back(SLOTS))
                    pool.sem_inc(gathers_begun, 1)
                    gather(g)
                if g.known and g.n == ACC_LAG:
                    pool.wait_ge(table_zeroed, 16 * (ZERO_PARTS + 2))
                if g.back(ACC_LAG).exists():
                    accumulate(g.back(ACC_LAG))

            for u in range(2 * UNROLL):
                step(Group(u // UNROLL, u % UNROLL))
            with pool.Fori(2, ITERS) as it:
                for u in range(UNROLL):
                    step(Group(it, u))
            for u in range(1 + ACC_LAG):
                step(Group(ITERS, u))
            pool.wait_ge(accumulated, 16 * ALL_TILES)

        @block.vector
        def _(dve):
            dve.memset(zeros[:, :], 0.0).then_inc(zeros_set, 1)
            dve.memset(w_e[:, :, :], 0.0).then_inc(w_cleared, 1)
            dve.wait_ge(ids_loaded, 96)
            dve.tensor_copy(gidx[:, 0, :, :], ids[:, :, 0:TILES]).then_inc(staged, 1)
            dve.memset(ones[:, :], 1.0)
            dve.memset(one_col[:, :], 1.0)
            dve.memset(eps_col[:, :], EPS).then_inc(consts, 1)
            dve.wait_ge(masks_made, 2)
            dve.tensor_reduce(small[:, 0:1], upto[:, :], AX.X, ALU.add).then_inc(prep, 1)
            dve.wait_ge(prep, 1)
            for j in range(TILES):
                dve.tensor_scalar(dump_row[:, j:j + 1], small[:, 0:1], float(NODES + P * j - 1), None, ALU.add)
            dve.tensor_scalar(small[:, 1:2], small[:, 0:1], float(E_REST) + 0.5, None, ALU.is_lt)
            dve.tensor_scalar(small[:, 2:3], small[:, 0:1], float(NODES + TILES * P - 1), None, ALU.add)
            dve.tensor_copy(src_f[:, :], ids[:, 0, :]).then_inc(prep, 1)
            dve.wait_ge(prep, 2)
            dve.tensor_scalar(real[:, :], ones[:, :], small[:, 1:2], None, ALU.mult)
            dve.tensor_tensor(small[:, 3:4], src_f[:, E_COLS:ALL_TILES], small[:, 2:3],
                              ALU.subtract).then_inc(prep, 1)
            dve.wait_ge(prep, 3)
            dve.tensor_scalar(src_f[:, E_COLS:ALL_TILES], small[:, 3:4], small[:, 1:2], small[:, 2:3],
                              ALU.mult, ALU.add).then_inc(prep, 1)
            dve.wait_ge(prep, 4)
            dve.tensor_copy(own[:, 0, :], src_f[:, 0:TILES]).then_inc(own_staged, 1)
            def stage_indices(g):
                dve.tensor_copy(gidx[:, g.slot(UNROLL), :, :],
                                ids[:, :, bass.ds(g.n * TILES, TILES)]).then_inc(staged, 1)
                wait_group(dve, target_done, g.back(UNROLL))
                dve.tensor_copy(own[:, g.slot(UNROLL), :],
                                src_f[:, bass.ds(g.n * TILES, TILES)]).then_inc(own_staged, 1)

            def sums(g):
                slot, rows = g.slot(SLOTS), slice(g.first_row, g.end_row)
                if g.exists():
                    dve.wait_ge(gathered[slot], 16 * GATHERED * g.uses(SLOTS) + 16 * GATHERED)
                if g.nodes():
                    extra = 16 * (X_LAST - 1) if g.known and g.n == STEPS - 1 else 0
                    dve.wait_ge(x_loaded[slot], 16 * (g.uses(SLOTS) - len(range(slot, SKEW, SLOTS))) + 16 + extra)
                wait_group(dve, centred, g.back(1))
                dve.tensor_reduce(row_sum[:, rows], xg[:, slot, rows, :], AX.X, ALU.add).then_inc(summed, 1)

            def centre(g):
                wait_group(dve, summed, g)
                if g.back(2).exists():
                    wait_group(dve, z_turned, g.back(2))
                wait_group(dve, y_done, g.back(2))
                rows = slice(g.first_row, g.end_row)
                dve.scalar_tensor_tensor(
                    out=xc[:, g.slot(2), rows, :],
                    in0=row_sum[:, rows].unsqueeze(2).to_broadcast([P, g.end_row - g.first_row, F]),
                    scalar=-1.0 / F, in1=xg[:, g.slot(SLOTS), rows, :], op0=ALU.mult, op1=ALU.add,
                ).then_inc(centred, 1)

            def sum_squares(g):
                wait_group(dve, squared, g)
                wait_group(dve, lnv_done, g.back(1))
                rows = slice(g.first_row, g.end_row)
                dve.tensor_reduce(row_ssq[:, rows], sq[:, rows, :], AX.X, ALU.add).then_inc(ssq_done, 1)

            def count_not_later(g):
                wait_group(dve, src_spread, g)
                wait_group(dve, later_done, g.back(1))
                for b in range(TILES):
                    ins = dve.scalar_tensor_tensor(
                        out=not_later[:, b, :], in0=ps_src[:, b, :], scalar=own[:, g.slot(UNROLL), b:b + 1],
                        in1=upto[:, :], op0=ALU.is_equal, op1=ALU.mult, accum_out=no_later[:, b:b + 1])
                ins.then_inc(not_later_done, 1)

            def targets(g):
                rows = own[:, g.slot(UNROLL), :]
                wait_group(dve, same_done, g)
                wait_group(dve, not_later_done, g)
                dve.tensor_tensor(later[:, :], matches[:, :], no_later[:, :], ALU.subtract).then_inc(later_done, 1)
                wait_group(dve, moved_done, g.back(1))
                dve.tensor_tensor(gap[:, :], dump_row[:, :], rows, ALU.subtract).then_inc(gap_done, 1)
                wait_group(dve, later_done, g)
                wait_group(dve, gap_done, g)
                wait_group(dve, target_done, g.back(1))
                dve.scalar_tensor_tensor(out=moved[:, :], in0=later[:, :], scalar=0.5, in1=gap[:, :],
                                         op0=ALU.is_gt, op1=ALU.mult).then_inc(moved_done, 1)
                wait_group(dve, moved_done, g)
                wait_group(dve, slots_free, g)
                dve.tensor_tensor(target[:, g.slot(UNROLL), :], moved[:, :], rows, ALU.add).then_inc(target_done, 1)

            def softplus(g):
                wait_group(dve, spl_done, g)
                wait_group(dve, msg_done, g.back(1))
                wait_group(dve, gate_done, g.back(1))
                dve.scalar_tensor_tensor(out=soft[:, :, :], in0=ps_v[g.slot(2)][:, :, :], scalar=0.0, in1=spl[:, :, :],
                                         op0=ALU.max, op1=ALU.add).then_inc(soft_done, 1)

            def normalise(g):
                wait_group(dve, rstd_done, g)
                rows = slice(g.first_row, g.end_row)
                h = xc[:, g.slot(2), rows, :]
                dve.scalar_tensor_tensor(out=h, in0=h, scalar=0.0,
                                         in1=row_rstd[:, rows].unsqueeze(2)
                                         .to_broadcast([P, g.end_row - g.first_row, F]),
                                         op0=ALU.max, op1=ALU.mult).then_inc(h_done, 1)

            def residual(g, spill):
                if not g.nodes():
                    dve.sem_inc(y_done, 1)
                    return
                wait_group(dve, h_done, g)
                if not spill:
                    dve.wait_ge(spilled, 16 * SPILL)
                row = (g.n - SKEW) * BULK - (0 if spill else SPILL * BULK)
                dve.tensor_tensor(y_kept[:, bass.ds(row, BULK), :], xc[:, g.slot(2), GATHERED:ROWS, :],
                                  xg[:, g.slot(SLOTS), GATHERED:ROWS, :], ALU.add).then_inc(y_done, 1)

            def message(g):
                wait_group(dve, gate_done, g)
                wait_group(dve, comb_done, g.back(1))
                dve.tensor_tensor(msg[:, :, :], gate[:, :, :], soft[:, :, F:2 * F], ALU.mult).then_inc(msg_done, 1)

            def step(g, spill):
                if g.back(3).exists():
                    message(g.back(3))
                if g.back(-1).exists():
                    stage_indices(g.back(-1))
                if in_steps(g.back(1)):
                    sum_squares(g.back(1))
                if in_steps(g):
                    sums(g)
                    centre(g)
                if in_steps(g.back(1)):
                    normalise(g.back(1))
                    residual(g.back(1), spill)
                if g.back(3).exists():
                    targets(g.back(3))
                if g.back(2).exists():
                    count_not_later(g.back(2))
                    softplus(g.back(2))

            step(Group(0, 0), True)
            dve.wait_ge(w_loaded, 16 * (4 + 2 * TILES + 2 * TILES))
            dve.tensor_scalar(w_z[:, 0:F], w_z[:, 0:F], -1.0, None, ALU.mult)
            dve.tensor_scalar(w_e[:, :, 0:F], w_e[:, :, 0:F], -1.0, None, ALU.mult)
            dve.tensor_scalar(b_row[:, :, 0:F], b_row[:, :, 0:F], -1.0, None, ALU.mult).then_inc(prep, 1)
            for u in range(1, UNROLL):
                step(Group(0, u), True)
            first_kept = (SPILL + 1 + SKEW) // UNROLL
            with dve.Fori(1, first_kept) as it:
                for u in range(UNROLL):
                    step(Group(it, u), True)
            with dve.Fori(first_kept, ITERS) as it:
                for u in range(UNROLL):
                    step(Group(it, u), False)
            for u in range(STEPS - LAST + 1):
                step(Group(ITERS, u), False)

        @block.scalar
        def _(act):
            act.preload_act_table_set("natural_log_exp_and_others")
            act.wait_ge(zeros_set, 1)
            whole = N_ROWS // BULK * BULK

            def zero_table(u):
                n = whole // ZERO_PARTS
                act.dma_start(m_rows[:, u * n:(u + 1) * n, :].rearrange("p (n r) f -> p n (r f)", r=BULK),
                              zeros[:, :].unsqueeze(1).to_broadcast([P, n // BULK, BULK * F])
                              ).then_inc(table_zeroed, 16)
                if u == ZERO_PARTS - 1:
                    act.dma_start(m_rows[:, whole:N_ROWS, :],
                                  zeros[:, 0:(N_ROWS - whole) * F].rearrange("p (r f) -> p r f", f=F)
                                  ).then_inc(table_zeroed, 16)
                    over = (N_REST + DUMP) // 96
                    act.dma_start(msgs[P * N_ROWS:NODES + DUMP, :].rearrange("(p r) f -> p (r f)", p=96),
                                  zeros[0:96, 0:over * F]).then_inc(table_zeroed, 16)

            act.wait_ge(consts, 1)

            def square(g):
                wait_group(act, centred, g)
                wait_group(act, ssq_done, g.back(1))
                rows = slice(g.first_row, g.end_row)
                act.activation(sq[:, rows, :], xc[:, g.slot(2), rows, :], ACT.Square).then_inc(squared, 1)

            def rstd(g):
                wait_group(act, ssq_done, g)
                wait_group(act, rstd_done, g.back(1))
                rows = slice(g.first_row, g.end_row)
                act.activation(row_lnv[:, rows], row_ssq[:, rows], ACT.Ln, bias=eps_col[:, 0:1],
                               scale=1.0 / F).then_inc(lnv_done, 1)
                wait_group(act, lnv_done, g)
                wait_group(act, h_done, g.back(1))
                act.activation(row_rstd[:, rows], row_lnv[:, rows], ACT.Exp, scale=-0.5).then_inc(rstd_done, 1)

            def gates(g):
                wait_group(act, soft_done, g)
                wait_group(act, msg_done, g.back(1))
                act.activation(gate[:, :, :], soft[:, :, 0:F], ACT.Exp, scale=-1.0).then_inc(gate_done, 1)

            def copy_turned(g):
                wait_group(act, ea_turned, g)
                wait_group(act, v_done, g.back(1))
                act.activation(ea_t[:, :], ps_e[:, :], ACT.Copy).then_inc(ea_copied, 1)
                wait_group(act, z_turned, g)
                act.activation(z_t[:, :, :], ps_z[:, :, :], ACT.Copy).then_inc(z_copied, 1)

            def softplus_log(g):
                wait_group(act, v_done, g)
                wait_group(act, soft_done, g.back(1))
                act.activation(spl[:, :, :], ps_v[g.slot(2)][:, :, :], ACT.Abs).then_inc(spl_steps, 1)
                act.wait_ge(spl_steps, 2 * g.n + 1)
                act.activation(spl[:, :, :], spl[:, :, :], ACT.Exp, scale=-1.0).then_inc(spl_steps, 1)
                act.wait_ge(spl_steps, 2 * g.n + 2)
                act.activation(spl[:, :, :], spl[:, :, :], ACT.Ln, bias=one_col[:, 0:1]).then_inc(spl_done, 1)

            def same_source(g):
                wait_group(act, src_spread, g)
                wait_group(act, comb_done, g.back(1))
                for b in range(TILES):
                    ins = act.activation(same[:, b, b:TILES, :], ps_src[:, b:TILES, :], ACT.Abs, scale=-1.0,
                                         bias=own[:, g.slot(UNROLL), b:b + 1])
                ins.then_inc(same_steps, 1)
                wait_group(act, same_steps, g)
                wait_group(act, later_done, g.back(1))
                for b in range(TILES):
                    ins = act.activation(same[:, b, b:TILES, :], same[:, b, b:TILES, :], ACT.Relu, scale=-1.0,
                                         bias=one_col[:, 0:1], accum_out=matches[:, b:b + 1])
                ins.then_inc(same_done, 1)

            def copy_comb(g):
                wait_group(act, comb_done, g)
                wait_group(act, slots_free, g)
                act.activation(comb[:, g.slot(UNROLL), :, :], ps_c[:, :, :], ACT.Copy).then_inc(comb_copied, 1)

            def spill(g):
                wait_group(act, y_done, g)
                row = (g.n - SKEW) * BULK
                act.dma_start(y_spill[:, bass.ds(row, BULK), :],
                              y_kept[:, bass.ds(row, BULK), :]).then_inc(spilled, 16)

            def step(g, spills):
                if in_steps(g.back(1)):
                    rstd(g.back(1))
                if g.back(2).exists():
                    softplus_log(g.back(2))
                if in_steps(g):
                    square(g)
                if g.back(1).exists():
                    copy_turned(g.back(1))
                if g.back(2).exists():
                    gates(g.back(2))
                if g.back(3).exists():
                    copy_comb(g.back(3))
                if g.back(2).exists():
                    same_source(g.back(2))
                if spills and g.back(1).nodes():
                    spill(g.back(1))

            for u in range(ZERO_AHEAD):
                zero_table(u)
            act.wait_ge(w_cleared, 1)
            for c, (w, b) in enumerate(((w_f, b_f), (w_s, b_s))):
                cols = slice(c * F, (c + 1) * F)
                act.dma_start(w_z[0:F, cols], w[0:F, :]).then_inc(w_loaded, 16)
                act.dma_start(w_z[F:2 * F, cols], w[F:2 * F, :]).then_inc(w_loaded, 16)
                for j in range(TILES):
                    act.dma_start(w_e[j * EF:(j + 1) * EF, j, cols], w[2 * F:2 * F + EF, :]).then_inc(w_loaded, 16)
                    act.dma_start(b_row[0:1, j, cols], b.rearrange("(a f) -> a f", a=1)).then_inc(w_loaded, 16)
            for u in range(UNROLL):
                for k in range(ZERO_AHEAD + 2 * u, min(ZERO_AHEAD + 2 * u + 2, ZERO_PARTS)):
                    zero_table(k)
                step(Group(0, u), True)
            first_kept = (SPILL + 1 + SKEW) // UNROLL
            with act.Fori(1, first_kept) as it:
                for u in range(UNROLL):
                    step(Group(it, u), True)
            with act.Fori(first_kept, ITERS) as it:
                for u in range(UNROLL):
                    step(Group(it, u), False)
            for u in range(STEPS - LAST + 1):
                step(Group(ITERS, u), False)
            act.activation(msg_sum[:, :], ps_sum[:, :], ACT.Copy).then_inc(sum_kept, 1)
            act.wait_ge(spilled, 16 * SPILL)

        @block.tensor
        def _(pe):
            pe.wait_ge(masks_made, 2)
            pe.wait_ge(consts, 1)
            pe.wait_ge(prep, 5)
            pe.matmul(ps_sum[:, :], zeros[:, 0:P], zeros[:, 0:F], start=True, stop=True,
                      skip_group_check=True).then_inc(sum_started, 1)

            def turn_edges(g):
                extra = 16 * (EA_LAST - 1) if g.known and g.n == LAST else 0
                pe.wait_ge(ea_loaded[g.slot(SLOTS)], 16 * g.uses(SLOTS) + 16 + extra)
                wait_group(pe, ea_copied, g.back(1))
                pe.transpose(ps_e[:, :], eas[:, g.slot(SLOTS), :, :].rearrange("p t f -> p (t f)"),
                             ident[:, :]).then_inc(ea_turned, 1)

            def spread_sources(g):
                wait_group(pe, same_done, g.back(1))
                wait_group(pe, not_later_done, g.back(1))
                wait_group(pe, own_staged, g)
                for j in range(TILES):
                    ins = pe.matmul(ps_src[:, j, :], own[:, g.slot(UNROLL), j:j + 1].to_broadcast([P, P]),
                                    ident[:, :], start=True, stop=True)
                ins.then_inc(src_spread, 1)

            def turn_z(g):
                wait_group(pe, h_done, g)
                wait_group(pe, z_copied, g.back(1))
                for j in range(TILES):
                    ins = pe.transpose(ps_z[:, j, :],
                                       xc[:, g.slot(2), 2 * j:2 * j + 2, :].rearrange("p c f -> p (c f)"),
                                       ident[:, :])
                ins.then_inc(z_turned, 1)

            def products(g):
                wait_group(pe, soft_done, g.back(2))
                v = ps_v[g.slot(2)]
                wait_group(pe, ea_copied, g)
                wait_group(pe, z_copied, g)
                pe.matmul(v[:, :, :].rearrange("p t f -> p (t f)"), ones[0:1, :],
                          b_row[0:1, :, :].rearrange("p t f -> p (t f)"), start=True, stop=True)
                for j in range(TILES):
                    pe.matmul(v[:, j, :], ea_t[:, :], w_e[:, j, :], start=False, stop=True,
                              skip_group_check=True)
                    ins = pe.matmul(v[:, j, :], z_t[:, j, :], w_z[:, :], start=False, stop=True,
                                    skip_group_check=True)
                ins.then_inc(v_done, 1)

            def combine(g):
                wait_group(pe, same_done, g)
                wait_group(pe, msg_done, g)
                wait_group(pe, comb_copied, g.back(1))
                for j in range(TILES):
                    for b in range(j + 1):
                        pe.matmul(ps_c[:, j, :], same[:, b, j, :], msg[:, b, :], start=(b == 0), stop=(b == j))
                last = g.known and g.n == LAST
                for j in range(TILES):
                    w = real if last and j == TILES - 1 else ones
                    ins = pe.matmul(ps_sum[:, :], w[:, :], msg[:, j, :], start=False, stop=True, skip_group_check=True)
                ins.then_inc(comb_done, 1)

            def step(g):
                if g.back(3).exists():
                    combine(g.back(3))
                if g.back(1).exists():
                    turn_edges(g.back(1))
                    turn_z(g.back(1))
                    products(g.back(1))
                    spread_sources(g.back(1))

            run_groups(pe, step, 3)


def stage_two(nc, sem, msgs, y_spill, gamma, beta, out, m_rows, out_rows, y_kept, ones, ident, eps_col, msg_sum):
    with ExitStack() as ctx:
        def sb(name, shape, dt=F32):
            return ctx.enter_context(nc.sbuf_tensor(name, shape, dt))

        m_buf = sb("m_buf", [P, M_BUFS, max(n for _, n in BLOCKS), F])
        m_rest = sb("m_rest", [N_REST, F])
        sq_acc = sb("sq_acc", [P, SQ_ROWS, F])
        sq_row = sb("sq_row", [P, F])
        gam = sb("gam", [P, F])
        bet = sb("bet", [P, F])
        mean = sb("mean", [P, F])
        mean2 = sb("mean2", [P, F])
        var = sb("var", [P, F])
        lnv = sb("lnv", [P, F])
        scale = sb("scale", [P, F])
        shift = sb("shift", [P, F])
        part = sb("part", [P, SPLIT, F], BF16)
        left = sb("left", [P, SPLIT, F])
        shift_row = sb("shift_row", [P, F], BF16)
        ones_b = sb("ones_b", [SPLIT, P], BF16)
        ps_all = ctx.enter_context(nc.psum_tensor("ps_all", [P, 2 * Y_ROWS, F], F32))
        ps_sq = [ps_all[:, i * SQ_ROWS:(i + 1) * SQ_ROWS, :] for i in range(SQ_BUFS)]
        ps_tot = ps_all[:, SQ_BUFS * SQ_ROWS, :]
        ps_y = [ps_all[:, i * Y_ROWS:(i + 1) * Y_ROWS, :] for i in range(2)]

        m_loaded = [sem(f"m_loaded{i}") for i in range(M_BUFS)]
        rest_loaded = sem("rest_loaded")
        affine_loaded = sem("affine_loaded")
        y_loaded = [sem(f"y_loaded{i}") for i in range(SPILLED_BLOCKS)]
        block_squared = sem("block_squared")
        part_squared = sem("part_squared")
        part_cleared = sem("part_cleared")
        part_added = sem("part_added")
        acc_reduced = sem("acc_reduced")
        total_ready = sem("total_ready")
        var_ready = sem("var_ready")
        ln_ready = sem("ln_ready")
        rstd_ready = sem("rstd_ready")
        chain = sem("chain")
        shift_ready = sem("shift_ready")
        split_done = sem("split_done")
        scaled = sem("scaled")
        y_summed = sem("y_summed")
        added = sem("added")
        rest_done = sem("rest_done")
        stored = [sem(f"stored{i}") for i in range(M_BUFS)]
        rest_stored = sem("rest_stored")

        parts = [(b, r, min(SQ_ROWS, n - r)) for b, (_, n) in enumerate(BLOCKS) for r in range(0, n, SQ_ROWS)]
        REST = -1
        parts.insert(parts.index((M_BUFS, 0, SQ_ROWS)), (REST, 0, 1))

        def rows_of(part, data):
            b, _, n = part
            return data[0:N_REST, 0:1, :] if b == REST else data[:, 0:n, :]
        held = list(range(NB - M_BUFS, NB))
        order = held + list(range(SPILLED_BLOCKS, NB - M_BUFS)) + list(range(SPILLED_BLOCKS))
        assert len(order) == NB
        rest_row = (LAST - SPILL) * BULK + LAST_ROWS

        def buf_of(i):
            return order[i] % M_BUFS if i < M_BUFS else order[i % M_BUFS] % M_BUFS

        def loads_of(i):
            b = buf_of(i)
            return len([k for k in range(NB) if k % M_BUFS == b]) + len(
                [k for k in range(M_BUFS, i + 1) if buf_of(k) == b])

        def stores_of(i):
            return len([k for k, _, _ in y_parts if k <= i and buf_of(k) == buf_of(i)])

        def y_of(b):
            r0, n = BLOCKS[b]
            if b >= SPILLED_BLOCKS:
                return y_kept[:, r0 - SPILL * BULK:r0 - SPILL * BULK + n, :]
            return y_kept[:, b * S_BLK:b * S_BLK + n, :]

        takes = {}
        for b in range(SPILLED_BLOCKS):
            lo, hi = b * S_BLK, b * S_BLK + BLOCKS[b][1]
            over = [i for i, k in enumerate(order) if k >= SPILLED_BLOCKS
                    and BLOCKS[k][0] - SPILL * BULK < hi and BLOCKS[k][0] - SPILL * BULK + BLOCKS[k][1] > lo]
            takes[b] = max(over)

        def part_rows(i):
            return Y_ROWS // 2 if i in (0, 1, NB - 1) else Y_ROWS

        y_parts = [(i, r, min(part_rows(i), BLOCKS[b][1] - r)) for i, b in enumerate(order)
                   for r in range(0, BLOCKS[b][1], part_rows(i))]

        def sums_of(i):
            return len([k for k, _, _ in y_parts if k <= i])

        block = ctx.enter_context(nc.Block())

        @block.sync
        def _(sp):
            for b, (r0, n) in enumerate(BLOCKS):
                if b == M_BUFS:
                    sp.dma_start(m_rest[:, :], msgs[P * N_ROWS:NODES, :]).then_inc(rest_loaded, 16)
                    for to, row in ((gam, gamma), (bet, beta)):
                        sp.dma_start(to[:, :], row.rearrange("(a f) -> a f", a=1).to_broadcast([P, F])
                                     ).then_inc(affine_loaded, 16)
                if b >= M_BUFS:
                    sp.wait_ge(block_squared, b - M_BUFS + 1)
                sp.dma_start(m_buf[:, b % M_BUFS, 0:n, :], m_rows[:, r0:r0 + n, :]).then_inc(m_loaded[b % M_BUFS], 16)
            for i in range(M_BUFS, NB):
                b = order[i]
                r0, n = BLOCKS[b]
                if b < SPILLED_BLOCKS:
                    sp.wait_ge(y_summed, sums_of(takes[b]))
                    sp.dma_start(y_of(b), y_spill[:, r0:r0 + n, :]).then_inc(y_loaded[b], 16)
                sp.wait_ge(stored[buf_of(i)], 16 * stores_of(i - M_BUFS))
                sp.dma_start(m_buf[:, buf_of(i), 0:n, :], m_rows[:, r0:r0 + n, :]).then_inc(m_loaded[buf_of(i)], 16)

        @block.scalar
        def _(act):
            for k, (b, r, n) in enumerate(parts):
                if k >= SQ_BUFS:
                    act.wait_ge(part_added, k - SQ_BUFS + 1)
                if b == REST:
                    act.wait_ge(rest_loaded, 16)
                    act.activation(ps_sq[k % SQ_BUFS][0:N_REST, 0, :], m_rest[:, :], ACT.Square
                                   ).then_inc(part_squared, 1)
                    continue
                if r == 0:
                    act.wait_ge(m_loaded[b % M_BUFS], 16 * (b // M_BUFS + 1))
                ins = act.activation(ps_sq[k % SQ_BUFS][:, 0:n, :], m_buf[:, b % M_BUFS, r:r + n, :], ACT.Square)
                ins.then_inc(part_squared, 1)
                if r + n == BLOCKS[b][1]:
                    act.wait_ge(part_squared, k + 1)
                    act.sem_inc(block_squared, 1)
            act.wait_ge(var_ready, 1)
            act.activation(lnv[:, :], var[:, :], ACT.Ln, bias=eps_col[:, 0:1]).then_inc(ln_ready, 1)
            act.wait_ge(ln_ready, 1)
            act.activation(var[:, :], lnv[:, :], ACT.Exp, scale=-0.5).then_inc(rstd_ready, 1)
            for k, (i, r, n) in enumerate(y_parts):
                r0 = BLOCKS[order[i]][0] + r
                act.wait_ge(added, k + 1)
                act.dma_start(out_rows[:, r0:r0 + n, :], m_buf[:, buf_of(i), r:r + n, :]).then_inc(stored[buf_of(i)], 16)
            act.wait_ge(rest_done, 3)
            act.dma_start(out[P * N_ROWS:NODES, :], m_rest[:, :]).then_inc(rest_stored, 16)
            for k in range(M_BUFS):
                last = max(i for i in range(NB) if buf_of(i) == k)
                act.wait_ge(stored[k], 16 * stores_of(last))
            act.wait_ge(rest_stored, 16)

        @block.tensor
        def _(pe):
            pe.wait_ge(acc_reduced, 1)
            pe.matmul(ps_tot, ones[:, :], sq_row[:, :], start=True, stop=True).then_inc(total_ready, 1)

            def add_rows(k):
                i, r, n = y_parts[k]
                for c in range(0, n, BANK_ROWS):
                    w = min(BANK_ROWS, n - c)
                    pe.matmul(ps_y[k % 2][:, c:c + w, :], ident[:, :], y_of(order[i])[:, r + c:r + c + w, :],
                              start=True, stop=False, skip_group_check=True)

            def add_shift(k):
                _, _, n = y_parts[k]
                for c in range(0, n, BANK_ROWS):
                    w = min(BANK_ROWS, n - c)
                    ins = pe.matmul(ps_y[k % 2][:, c:c + w, :], ones_b[:, :],
                                    shift_row[0:SPLIT, :].unsqueeze(1).to_broadcast([SPLIT, w, F]),
                                    start=False, stop=True, skip_group_check=True)
                ins.then_inc(y_summed, 1)

            pe.wait_ge(var_ready, 1)
            add_rows(0)
            pe.wait_ge(split_done, SPLIT)
            add_shift(0)
            add_rows(1)
            add_shift(1)
            for k in range(2, len(y_parts)):
                b = order[y_parts[k][0]]
                if b < SPILLED_BLOCKS:
                    pe.wait_ge(y_loaded[b], 16)
                pe.wait_ge(added, k - 1)
                add_rows(k)
                add_shift(k)

        @block.vector
        def _(dve):
            dve.memset(ones_b[:, :], 1.0)
            dve.memset(sq_acc[:, :, :], 0.0).then_inc(part_cleared, 1)
            dve.wait_ge(part_cleared, 1)
            for k, part_k in enumerate(parts):
                dve.wait_ge(part_squared, k + 1)
                if k:
                    dve.wait_ge(part_added, k)
                total = rows_of(part_k, sq_acc)
                dve.tensor_tensor(total, total, rows_of(part_k, ps_sq[k % SQ_BUFS]), ALU.add).then_inc(part_added, 1)
            dve.wait_ge(part_added, len(parts))
            dve.tensor_reduce(sq_row[:, :], sq_acc[:, :, :].rearrange("p r f -> p f r"), AX.X,
                              ALU.add).then_inc(acc_reduced, 1)
            dve.tensor_scalar(mean[:, :], msg_sum[:, :], 1.0 / NODES, None, ALU.mult).then_inc(chain, 1)
            dve.wait_ge(chain, 1)
            dve.tensor_tensor(mean2[:, :], mean[:, :], mean[:, :], ALU.mult).then_inc(chain, 1)
            dve.wait_ge(chain, 2)
            dve.wait_ge(total_ready, 1)
            dve.scalar_tensor_tensor(out=var[:, :], in0=ps_tot, scalar=1.0 / NODES, in1=mean2[:, :],
                                     op0=ALU.mult, op1=ALU.subtract).then_inc(var_ready, 1)
            dve.wait_ge(rstd_ready, 1)
            dve.wait_ge(affine_loaded, 32)
            dve.tensor_tensor(scale[:, :], var[:, :], gam[:, :], ALU.mult).then_inc(chain, 1)
            dve.wait_ge(chain, 3)
            dve.tensor_tensor(mean2[:, :], mean[:, :], scale[:, :], ALU.mult).then_inc(chain, 1)
            dve.wait_ge(chain, 4)
            dve.tensor_tensor(shift[:, :], bet[:, :], mean2[:, :], ALU.subtract).then_inc(shift_ready, 1)
            dve.wait_ge(shift_ready, 1)

            for k in range(SPLIT):
                dve.tensor_copy(part[:, k, :], shift[:, :] if k == 0 else left[:, k, :]).then_inc(chain, 1)
                dve.wait_ge(chain, 5 + 2 * k)
                if k < SPLIT - 1:
                    dve.tensor_tensor(left[:, k + 1, :], shift[:, :] if k == 0 else left[:, k, :], part[:, k, :],
                                      ALU.subtract).then_inc(chain, 1)
                    dve.wait_ge(chain, 6 + 2 * k)
            for k in range(SPLIT):
                if k == 0:
                    ins = dve.tensor_scalar(shift_row[:, :], part[:, k, :], ident[:, k:k + 1], None, ALU.mult)
                else:
                    ins = dve.scalar_tensor_tensor(out=shift_row[:, :], in0=part[:, k, :], scalar=ident[:, k:k + 1],
                                                   in1=shift_row[:, :], op0=ALU.mult, op1=ALU.add)
                ins.then_inc(split_done, 1)
                dve.wait_ge(split_done, k + 1)

            for k, (i, r, n) in enumerate(y_parts):
                m = m_buf[:, buf_of(i), r:r + n, :]
                dve.wait_ge(m_loaded[buf_of(i)], 16 * loads_of(i))
                dve.tensor_tensor(m, m, scale[:, :].unsqueeze(1).to_broadcast([P, n, F]), ALU.mult).then_inc(scaled, 1)
                dve.wait_ge(scaled, k + 1)
                dve.wait_ge(y_summed, k + 1)
                dve.tensor_tensor(m, m, ps_y[k % 2][:, 0:n, :], ALU.add).then_inc(added, 1)

            dve.tensor_tensor(m_rest[:, :], m_rest[:, :], scale[0:N_REST, :], ALU.mult).then_inc(rest_done, 1)
            dve.wait_ge(rest_done, 1)
            dve.tensor_tensor(m_rest[:, :], m_rest[:, :], y_kept[0:N_REST, rest_row, :], ALU.add).then_inc(rest_done, 1)
            dve.wait_ge(rest_done, 2)
            dve.tensor_tensor(m_rest[:, :], m_rest[:, :], shift[0:N_REST, :], ALU.add).then_inc(rest_done, 1)


_INS = ["x", "src", "dst", "edge_attr_32", "L0_gnn_W_f", "L0_gnn_b_f", "L0_gnn_W_s", "L0_gnn_b_s",
        "L0_gnn_gamma", "L0_gnn_beta"]


def kernel(**inputs):
    import numpy as _np
    import concourse.bacc as _bacc
    from concourse.bass_utils import run_bass_kernel_spmd as _run

    nc = _bacc.Bacc("TRN2", target_bir_lowering=False, num_devices=1)
    arrays, args = {}, []
    for name in _INS:
        a = _np.ascontiguousarray(inputs[name])
        arrays[f"in_{name}_dram"] = a
        args.append(nc.dram_tensor(f"in_{name}_dram", a.shape, mybir.dt.from_np(a.dtype), kind="ExternalInput").ap())
    out = nc.dram_tensor("out_dram", (NODES, F), F32, kind="ExternalOutput").ap()
    msgs = nc.dram_tensor("msgs_dram", (NODES + DUMP, F), F32, kind="Internal").ap()
    y_spill = nc.dram_tensor("y_spill_dram", (P, SPILL * BULK, F), F32, kind="Internal").ap()
    build(nc, *args, out, msgs, y_spill)
    r = _run(nc, [arrays], core_ids=[0])
    return r.results[0]["out_dram"]
```
